# Optimizing a Trainium2 kernel written in Bass

```python
import numpy as np
import jax
import jax.numpy as jnp

def _softmax(x, axis=-1):
    return jax.nn.softmax(x, axis=axis)

def _gelu(x):
    return jax.nn.gelu(x, approximate=True)

def _silu(x):
    return jax.nn.silu(x)

def _sigmoid(x):
    return jax.nn.sigmoid(x)

def _layernorm(x, axis=-1, eps=1e-05):
    m = jnp.mean(x, axis=axis, keepdims=True)
    v = jnp.var(x, axis=axis, keepdims=True)
    return (x - m) / jnp.sqrt(v + eps)

def _scatter_add(tgt, idx, src, axis=0):
    return tgt.at[idx].add(src)

def _segment_sum(src, seg, n):
    return jax.ops.segment_sum(src, seg, n)
kernel_name = 'mk_gnn_preln_d4_gnn_r32_ed6efc'

def setup_inputs(seed: int=0):
    np.random.seed(seed)
    _w = jnp.asarray

    def _rec_inputs():
        import jax
        import jax.numpy as jnp
        _gk = jax.random.key(seed)
        x = -0.0003713 + 1 * jax.random.normal(jax.random.fold_in(_gk, 1), (3125, 128), jnp.float32)
        src = jax.random.randint(jax.random.fold_in(_gk, 2), (100000,), 0, 3125, jnp.int32)
        dst = jnp.minimum((3125 * jax.random.uniform(jax.random.fold_in(_gk, 3), (100000,)) ** 2.0).astype(jnp.int32), 99999)
        _o = jnp.argsort(dst, stable=True)
        src = src[_o]
        dst = dst[_o]
        edge_type_8 = jax.random.randint(jax.random.fold_in(_gk, 13), (100000,), 0, 8, jnp.int32)
        edge_weight = jax.random.uniform(jax.random.fold_in(_gk, 14), (100000,), jnp.float32, 0.0, 1)
        return (x, src, dst, edge_type_8, edge_weight)
    x, src, dst, edge_type_8, edge_weight = _rec_inputs()

    def _L0_gnn_setup():
        import jax, jax.numpy as jnp
        import numpy as np
        N = 3125
        E = 50000
        D_IN = 128
        D_H = 128
        D_OUT = 128

        def _init_linear(key, out_dim, in_dim):
            bound = 1.0 / np.sqrt(in_dim)
            return jax.random.uniform(key, (out_dim, in_dim), jnp.float32, -bound, bound)

        def _sage_conv(x, src, dst, Wl, bl, Wr):
            msg = x[src]
            agg = jax.ops.segment_sum(msg, dst, num_segments=N)
            deg = jax.ops.segment_sum(jnp.ones((src.shape[0],), x.dtype), dst, num_segments=N)
            mean = agg / jnp.maximum(deg, 1.0)[:, None]
            return mean @ Wl.T + bl + x @ Wr.T
        key = jax.random.key(seed)
        ks = jax.random.split(key, 12)
        x = jax.random.normal(ks[0], (N, D_IN), jnp.float32)
        edge_index = jax.random.randint(ks[1], (2, E), 0, N, jnp.int32)
        dims = [(D_H, D_IN), (D_H, D_H), (D_OUT, D_H)]
        inp = {'x': x, 'edge_index': edge_index}
        for i, (do, di) in enumerate(dims):
            inp[f'Wl{i}'] = _init_linear(ks[2 + 3 * i], do, di)
            inp[f'bl{i}'] = jnp.zeros((do,), jnp.float32)
            inp[f'Wr{i}'] = _init_linear(ks[3 + 3 * i], do, di)
        return inp
    _L0_gnn_all = _L0_gnn_setup()
    _L0_gnn_in = {k: v for k, v in _L0_gnn_all.items() if k in ('Wl0', 'bl0', 'Wr0', 'Wl1', 'bl1', 'Wr1', 'Wl2', 'bl2', 'Wr2')}
    del _L0_gnn_all

    def _L1_gnn_setup():
        import jax, jax.numpy as jnp
        import numpy as np
        N_NODES = 3125
        N_EDGES = 18750
        H = 128
        T = 8
        L = 2

        def _gru_cell(x, h, wih, whh, bih, bhh):
            gi = x @ wih.T + bih
            gh = h @ whh.T + bhh
            i_r, i_z, i_n = jnp.split(gi, 3, axis=-1)
            h_r, h_z, h_n = jnp.split(gh, 3, axis=-1)
            r = jax.nn.sigmoid(i_r + h_r)
            z = jax.nn.sigmoid(i_z + h_z)
            n = jnp.tanh(i_n + r * h_n)
            return (1.0 - z) * n + z * h
        key = jax.random.key(seed)
        ks = jax.random.split(key, 12)
        s = 1.0 / np.sqrt(H)
        inp = {'node_features': jax.random.normal(ks[0], (N_NODES, H), dtype=jnp.float32), 'edge_index': jax.random.randint(ks[1], (2, N_EDGES), 0, N_NODES, dtype=jnp.int64), 'edge_type': jax.random.randint(ks[2], (N_EDGES,), 0, T, dtype=jnp.int64), 'node_proj_w': jax.random.uniform(ks[3], (H, H), jnp.float32, -s, s), 'node_proj_b': jax.random.uniform(ks[4], (H,), jnp.float32, -s, s), 'edge_W': jax.random.uniform(ks[5], (L, T, H, H), jnp.float32, -s, s), 'edge_b': jax.random.uniform(ks[6], (L, T, H), jnp.float32, -s, s), 'gru_wih': jax.random.uniform(ks[7], (L, 3 * H, H), jnp.float32, -s, s), 'gru_whh': jax.random.uniform(ks[8], (L, 3 * H, H), jnp.float32, -s, s), 'gru_bih': jax.random.uniform(ks[9], (L, 3 * H), jnp.float32, -s, s), 'gru_bhh': jax.random.uniform(ks[10], (L, 3 * H), jnp.float32, -s, s), 'out_w': jax.random.uniform(ks[11], (H, H), jnp.float32, -s, s), 'out_b': jnp.zeros((H,), jnp.float32)}
        return inp
    _L1_gnn_all = _L1_gnn_setup()
    _L1_gnn_in = {k: v for k, v in _L1_gnn_all.items() if k in ('node_proj_w', 'node_proj_b', 'edge_W', 'edge_b', 'gru_wih', 'gru_whh', 'gru_bih', 'gru_bhh', 'out_w', 'out_b')}
    del _L1_gnn_all

    def _L2_gnn_setup():
        import jax, jax.numpy as jnp
        import numpy as np
        N_NODES = 3125
        N_EDGES = 50000
        D = 128
        N_LAYERS = 3

        def _sage_layer(x, src, dst, wl, wr, b):
            msg = x[src]
            agg = jax.ops.segment_sum(msg, dst, num_segments=N_NODES)
            cnt = jax.ops.segment_sum(jnp.ones((src.shape[0],), x.dtype), dst, num_segments=N_NODES)
            mean = agg / jnp.maximum(cnt, 1.0)[:, None]
            return mean @ wl + x @ wr + b
        key = jax.random.key(seed)
        k_x, k_e, k_wl, k_wr = jax.random.split(key, 4)
        x = jax.random.normal(k_x, (N_NODES, D), dtype=jnp.float32)
        edge_index = jax.random.randint(k_e, (2, N_EDGES), 0, N_NODES, dtype=jnp.int64)
        scale = 1.0 / np.sqrt(D)
        Wl = jax.random.uniform(k_wl, (N_LAYERS, D, D), jnp.float32, -scale, scale)
        Wr = jax.random.uniform(k_wr, (N_LAYERS, D, D), jnp.float32, -scale, scale)
        b = jnp.zeros((N_LAYERS, D), jnp.float32)
        return {'x': x, 'edge_index': edge_index, 'Wl': Wl, 'Wr': Wr, 'b': b}
    _L2_gnn_all = _L2_gnn_setup()
    _L2_gnn_in = {k: v for k, v in _L2_gnn_all.items() if k in ('Wl', 'Wr', 'b')}
    del _L2_gnn_all

    def _L3_gnn_setup():
        import jax, jax.numpy as jnp
        import numpy as np
        N_NODES = 3125
        key = jax.random.key(seed)
        k1, k2, k3, k4, k5 = jax.random.split(key, 5)
        node_emb = jax.random.normal(k1, (3125, 128), dtype=jnp.float32)
        edge_weight = jax.random.uniform(k2, (50000,), dtype=jnp.float32)
        src = jax.random.randint(k3, (50000,), 0, 3125, dtype=jnp.int32)
        dst = jax.random.randint(k4, (50000,), 0, 3125, dtype=jnp.int32)
        W = jax.random.normal(k5, (128, 128), dtype=jnp.float32) * (1.0 / np.sqrt(128))
        return {'node_emb': node_emb, 'edge_weight': edge_weight, 'src': src, 'dst': dst, 'W': W}
    _L3_gnn_all = _L3_gnn_setup()
    _L3_gnn_in = {k: v for k, v in _L3_gnn_all.items() if k in ('W',)}
    del _L3_gnn_all
    return {'x': x, 'src': src, 'dst': dst, 'edge_type_8': edge_type_8, 'edge_weight': edge_weight, 'L0_gnn_Wl0': _L0_gnn_in['Wl0'], 'L0_gnn_bl0': _L0_gnn_in['bl0'], 'L0_gnn_Wr0': _L0_gnn_in['Wr0'], 'L0_gnn_Wl1': _L0_gnn_in['Wl1'], 'L0_gnn_bl1': _L0_gnn_in['bl1'], 'L0_gnn_Wr1': _L0_gnn_in['Wr1'], 'L0_gnn_Wl2': _L0_gnn_in['Wl2'], 'L0_gnn_bl2': _L0_gnn_in['bl2'], 'L0_gnn_Wr2': _L0_gnn_in['Wr2'], 'L1_gnn_node_proj_w': _L1_gnn_in['node_proj_w'], 'L1_gnn_node_proj_b': _L1_gnn_in['node_proj_b'], 'L1_gnn_edge_W': _L1_gnn_in['edge_W'], 'L1_gnn_edge_b': _L1_gnn_in['edge_b'], 'L1_gnn_gru_wih': _L1_gnn_in['gru_wih'], 'L1_gnn_gru_whh': _L1_gnn_in['gru_whh'], 'L1_gnn_gru_bih': _L1_gnn_in['gru_bih'], 'L1_gnn_gru_bhh': _L1_gnn_in['gru_bhh'], 'L1_gnn_out_w': _L1_gnn_in['out_w'], 'L1_gnn_out_b': _L1_gnn_in['out_b'], 'L2_gnn_Wl': _L2_gnn_in['Wl'], 'L2_gnn_Wr': _L2_gnn_in['Wr'], 'L2_gnn_b': _L2_gnn_in['b'], 'L3_gnn_W': _L3_gnn_in['W']}

def reference(x, src, dst, edge_type_8, edge_weight, L0_gnn_Wl0, L0_gnn_bl0, L0_gnn_Wr0, L0_gnn_Wl1, L0_gnn_bl1, L0_gnn_Wr1, L0_gnn_Wl2, L0_gnn_bl2, L0_gnn_Wr2, L1_gnn_node_proj_w, L1_gnn_node_proj_b, L1_gnn_edge_W, L1_gnn_edge_b, L1_gnn_gru_wih, L1_gnn_gru_whh, L1_gnn_gru_bih, L1_gnn_gru_bhh, L1_gnn_out_w, L1_gnn_out_b, L2_gnn_Wl, L2_gnn_Wr, L2_gnn_b, L3_gnn_W):
    import jax
    import jax.numpy as jnp

    def _L0_gnn_ref(x, edge_index, Wl0, bl0, Wr0, Wl1, bl1, Wr1, Wl2, bl2, Wr2):
        import jax, jax.numpy as jnp
        import numpy as np
        N = 3125
        E = 50000
        D_IN = 128
        D_H = 128
        D_OUT = 128

        def _init_linear(key, out_dim, in_dim):
            bound = 1.0 / np.sqrt(in_dim)
            return jax.random.uniform(key, (out_dim, in_dim), jnp.float32, -bound, bound)

        def _sage_conv(x, src, dst, Wl, bl, Wr):
            msg = x[src]
            agg = jax.ops.segment_sum(msg, dst, num_segments=N)
            deg = jax.ops.segment_sum(jnp.ones((src.shape[0],), x.dtype), dst, num_segments=N)
            mean = agg / jnp.maximum(deg, 1.0)[:, None]
            return mean @ Wl.T + bl + x @ Wr.T
        src, dst = (edge_index[0], edge_index[1])
        h = jax.nn.relu(_sage_conv(x, src, dst, Wl0, bl0, Wr0))
        h = jax.nn.relu(_sage_conv(h, src, dst, Wl1, bl1, Wr1))
        return _sage_conv(h, src, dst, Wl2, bl2, Wr2)

    def _L1_gnn_ref(node_features, edge_index, edge_type, node_proj_w, node_proj_b, edge_W, edge_b, gru_wih, gru_whh, gru_bih, gru_bhh, out_w, out_b):
        import jax, jax.numpy as jnp
        import numpy as np
        N_NODES = 3125
        N_EDGES = 18750
        H = 128
        T = 8
        L = 2

        def _gru_cell(x, h, wih, whh, bih, bhh):
            gi = x @ wih.T + bih
            gh = h @ whh.T + bhh
            i_r, i_z, i_n = jnp.split(gi, 3, axis=-1)
            h_r, h_z, h_n = jnp.split(gh, 3, axis=-1)
            r = jax.nn.sigmoid(i_r + h_r)
            z = jax.nn.sigmoid(i_z + h_z)
            n = jnp.tanh(i_n + r * h_n)
            return (1.0 - z) * n + z * h
        num_nodes = node_features.shape[0]
        src, dst = (edge_index[0], edge_index[1])
        h = jax.nn.relu(node_features @ node_proj_w.T + node_proj_b)
        for l in range(L):
            trans = jnp.einsum('nh,tdh->tnd', h, edge_W[l])
            msgs = trans[edge_type, src]
            agg = jax.ops.segment_sum(msgs, dst, num_segments=num_nodes)
            h = _gru_cell(agg, h, gru_wih[l], gru_whh[l], gru_bih[l], gru_bhh[l])
            h = jax.nn.relu(h)
        return h @ out_w.T + out_b

    def _L2_gnn_ref(x, edge_index, Wl, Wr, b):
        import jax, jax.numpy as jnp
        import numpy as np
        N_NODES = 3125
        N_EDGES = 50000
        D = 128
        N_LAYERS = 3

        def _sage_layer(x, src, dst, wl, wr, b):
            msg = x[src]
            agg = jax.ops.segment_sum(msg, dst, num_segments=N_NODES)
            cnt = jax.ops.segment_sum(jnp.ones((src.shape[0],), x.dtype), dst, num_segments=N_NODES)
            mean = agg / jnp.maximum(cnt, 1.0)[:, None]
            return mean @ wl + x @ wr + b
        src, dst = (edge_index[0], edge_index[1])
        h = x
        for i in range(N_LAYERS - 1):
            h = jax.nn.relu(_sage_layer(h, src, dst, Wl[i], Wr[i], b[i]))
        h = _sage_layer(h, src, dst, Wl[-1], Wr[-1], b[-1])
        return h

    def _L3_gnn_ref(node_emb, edge_weight, src, dst, W):
        import jax, jax.numpy as jnp
        import numpy as np
        N_NODES = 3125
        msg = node_emb[src] * edge_weight[:, None]
        agg = jax.ops.segment_sum(msg, dst, num_segments=N_NODES)
        return agg @ W.T
    edge_index = jnp.stack([src, dst])
    h = jnp.maximum(_layernorm(x, axis=-1), 0.0)
    x = x + _L0_gnn_ref(h, edge_index, L0_gnn_Wl0, L0_gnn_bl0, L0_gnn_Wr0, L0_gnn_Wl1, L0_gnn_bl1, L0_gnn_Wr1, L0_gnn_Wl2, L0_gnn_bl2, L0_gnn_Wr2)
    h = jnp.maximum(_layernorm(x, axis=-1), 0.0)
    x = x + _L1_gnn_ref(h, edge_index, edge_type_8, L1_gnn_node_proj_w, L1_gnn_node_proj_b, L1_gnn_edge_W, L1_gnn_edge_b, L1_gnn_gru_wih, L1_gnn_gru_whh, L1_gnn_gru_bih, L1_gnn_gru_bhh, L1_gnn_out_w, L1_gnn_out_b)
    h = jnp.maximum(_layernorm(x, axis=-1), 0.0)
    x = x + _L2_gnn_ref(h, edge_index, L2_gnn_Wl, L2_gnn_Wr, L2_gnn_b)
    h = jnp.maximum(_layernorm(x, axis=-1), 0.0)
    x = x + _L3_gnn_ref(h, edge_weight, src, dst, L3_gnn_W)
    return x

_drawn_inputs = setup_inputs


def setup_inputs(seed=0):
    import zlib

    import numpy as np

    out = dict(_drawn_inputs(seed))
    spreads = {'L0_gnn_bl0': (0.0, 0.325),
     'L0_gnn_bl1': (0.0, 0.1),
     'L0_gnn_bl2': (0.0, 0.1),
     'L1_gnn_out_b': (0.0, 0.1),
     'L2_gnn_b': (0.0, 0.1)}
    factors = {'L1_gnn_node_proj_b': 4.556,
     'L1_gnn_gru_whh': 3.201,
     'L1_gnn_gru_bih': 4.441,
     'L1_gnn_gru_bhh': 8.0}
    for name, (base, spread) in spreads.items():
        noise = np.random.default_rng([zlib.crc32(name.encode()), seed]).standard_normal(out[name].shape)
        drawn = base * np.exp(spread * noise) if base else spread * noise
        out[name] = jnp.asarray(drawn.astype(out[name].dtype))
    for name, factor in factors.items():
        out[name] = (out[name] * factor).astype(out[name].dtype)
    return out
```

```python
from contextlib import ExitStack

import concourse.bass as bass
from concourse import mybir

F32 = mybir.dt.float32
BF16 = mybir.dt.bfloat16
I32 = mybir.dt.int32
U32 = mybir.dt.uint32
ALU = mybir.AluOpType
ACT = mybir.ActivationFunctionType
AX = mybir.AxisListType

N, E, H, T = 3125, 100000, 128, 8
PT = 125
NB = N // PT
NTILE = E // PT
G = 8
NG = NTILE // G
EPS = 1e-5
CHUNKS = [(4 * j, min(4, NB - 4 * j)) for j in range((NB + 3) // 4)]
NC = len(CHUNKS)
BANK = 512

DEG, SAGE, TYPED, WEIGHTED = "deg", "sage", "typed", "weighted"
ROUNDS = [DEG, SAGE, SAGE, SAGE, TYPED, TYPED, SAGE, SAGE, SAGE, WEIGHTED]


def gnn_program(nc, a, out):
    ctx = ExitStack()
    with ctx:
        def sb(name, shape, dt=F32):
            return ctx.enter_context(nc.sbuf_tensor(name, shape, dt))

        def sem(name):
            return ctx.enter_context(nc.semaphore(name))

        def sems(name, keys):
            return {k: sem(f"{name}{k}") for k in keys}

        node_table = nc.dram_tensor("node_table", (N, H), F32).ap()
        typed_table = nc.dram_tensor("typed_table", (N * T, H), F32).ap()
        bound_scratch = nc.dram_tensor("bound_scratch", (NG, 2), I32).ap()

        dst_i = sb("dst_i", [PT, NTILE], I32)
        src_i = sb("src_i", [PT, NTILE], I32)
        typ_i = sb("typ_i", [PT, NTILE], I32)
        dst_f = sb("dst_f", [PT, NTILE])
        typed_i = sb("typed_i", [PT, NTILE], I32)
        scaled_src = sb("scaled_src", [PT, NTILE])
        weight = sb("weight", [PT, NTILE])
        dst_rows = sb("dst_rows", [NG, G * PT], I32)
        bound_f = sb("bound_f", [NG, 2])
        bound_i = sb("bound_i", [NG, 2], I32)
        bounds = sb("bounds", [1, 2 * NG], I32)
        node_id = sb("node_id", [PT, N])
        ring = sb("ring", [PT, 2 * G], U32)
        msg = sb("msg", [PT, 2 * G, H])
        onehot = sb("onehot", [PT, 2 * G, PT])
        x_rows = sb("x_rows", [PT, NB, H])
        h_rows = sb("h_rows", [PT, NB, H])
        hT = [sb(f"hT{i}", [H, N]) for i in range(2)]
        aggT = sb("aggT", [H, N])
        rdeg = sb("rdeg", [H, N])
        table_stage = sb("table_stage", [PT, 2, T * H])
        gate_r = sb("gate_r", [H, 2, 4 * PT])
        gate_z = sb("gate_z", [H, 2, 4 * PT])
        gate_n = sb("gate_n", [H, 2, 4 * PT])
        stats = sb("stats", [PT, NB, 6])
        moments = sb("moments", [PT, NB, 2])
        std = sb("std", [PT, NB])
        rstd = sb("rstd", [PT, NB])
        w_sage = sb("w_sage", [H, 12, H])
        b_col = sb("b_col", [H, 5])
        b_row = sb("b_row", [1, 3 * H])
        w_typed = sb("w_typed", [H, 2 * T * H])
        w_gru = sb("w_gru", [H, 2, 2, 3 * H])
        b_gru = sb("b_gru", [H, 2, 2, 3])
        b_rz = sb("b_rz", [H, 2, 2])
        w_misc = sb("w_misc", [H, 3, H])
        ones = sb("ones", [PT, H])
        eps_col = sb("eps_col", [PT, 1])
        zeros = sb("zeros", [1, BANK], BF16)
        ident = sb("ident", [H, H])

        psum = ctx.enter_context(nc.psum_tensor("psum", [H, 8 * BANK], F32))

        def bank(j):
            return psum[:, j * BANK:(j + 1) * BANK]

        def acc(j):
            n = CHUNKS[j][1]
            return bank(j)[:, 0:n * H].rearrange("p (b c) -> p b c", c=H)[:, :, 0:PT]

        def cols(t, j):
            b, n = CHUNKS[j]
            return t[:, b * PT:(b + n) * PT]

        def cols3(t, j):
            return cols(t, j).rearrange("p (b c) -> p b c", c=PT)

        spare = bank(7)[0:1, BANK - 1:BANK]
        NR = len(ROUNDS)
        gather_rounds = [r for r in range(NR) if ROUNDS[r] != DEG]
        first = {"L0": 1, "L1": 4, "L2": 6, "L3": 9}

        s_edges, s_x, s_weights, s_bounds = sem("s_edges"), sem("s_x"), sem("s_weights"), sem("s_bounds")
        s_bound_out, s_bound_in = sem("s_bound_out"), sem("s_bound_in")
        s_const = sem("s_const")
        s_ident = sem("s_ident")
        s_ids = sem("s_ids")
        s_typed_idx = sem("s_typed_idx")
        s_dve, s_act = sem("s_dve"), sem("s_act")
        s_ring = sem("s_ring")
        s_free = [sem(f"s_free{h}") for h in range(2)]
        s_onehot = [sem(f"s_onehot{h}") for h in range(2)]
        s_onehot_used = [sem(f"s_onehot_used{h}") for h in range(2)]
        s_gathered = {r: [sem(f"s_gathered{r}_{h}") for h in range(2)] for r in gather_rounds}
        s_table = sems("s_table", gather_rounds)
        s_summed = sems("s_summed", range(NR))
        s_typed_out = {r: [sem(f"s_typed_out{r}_{q}") for q in range(2)] for r in (4, 5)}
        s_evac = sems("s_evac", range(NR))
        s_lin = sems("s_lin", range(NR))
        s_new = sems("s_new", range(NR))
        s_trans = sems("s_trans", range(NR))
        s_rows = sems("s_rows", range(NR))
        s_var = sems("s_var", range(4))
        s_std = sems("s_std", range(4))
        s_norm = sems("s_norm", range(4))
        s_normT = sems("s_normT", range(3))
        s_normed = sems("s_normed", range(3))
        s_proj, s_projed = sem("s_proj"), sem("s_projed")
        s_tab, s_tab_a, s_tab_v = (sems(n, range(2)) for n in ("s_tab", "s_tab_a", "s_tab_v"))
        s_act1, s_dve1, s_act2 = (sems(n, range(2)) for n in ("s_act1_", "s_dve1_", "s_act2_"))
        s_fin = sems("s_fin", range(4))
        s_res = sems("s_res", range(4))
        s_out = sem("s_out")

        block = ctx.enter_context(nc.Block())

        hT_of = {1: 0, 2: 1, 3: 0, 4: 1, 5: 0, 6: 0, 7: 1, 8: 0}
        LAST = {"L0": 3, "L1": 5, "L2": 8, "L3": 9}
        layer_of = {LAST[k]: n for n, k in enumerate(LAST)}
        sage_w = {1: 0, 2: 2, 3: 4, 6: 6, 7: 8, 8: 10}
        bias_col = {1: 0, 2: 1, 6: 2, 7: 3}
        bias_row = {3: 0, 8: 1}

        @block.sync
        def _(sp):
            sp.dma_start(dst_rows[:], a["dst_rows"]).then_inc(s_bounds, 16)
            sp.dma_start(dst_i[:], a["dst_t"]).then_inc(s_edges, 16)
            sp.dma_start(src_i[:], a["src_t"]).then_inc(s_edges, 16)
            sp.dma_start(x_rows[:], a["x"].rearrange("(t p) f -> p t f", p=PT)).then_inc(s_x, 16)
            sp.dma_start(typ_i[:], a["typ_t"]).then_inc(s_edges, 16)
            sp.dma_start(weight[:], a["weight_t"]).then_inc(s_edges, 16)
            sp.wait_ge(s_typed_idx, 1)
            sp.dma_start(bound_scratch, bound_i[:]).then_inc(s_bound_out, 16)
            sp.wait_ge(s_bound_out, 16)
            sp.dma_start(bounds[:], bound_scratch.rearrange("(a g) c -> a (g c)", a=1)).then_inc(s_bound_in, 16)

            def store_norm(n, r):
                sp.wait_ge(s_norm[n], 1)
                sp.dma_start(node_table.rearrange("(t p) f -> p t f", p=PT), h_rows[:]).then_inc(s_table[r], 16)

            def store_rows(r):
                for j, (b, n) in enumerate(CHUNKS):
                    sp.wait_ge(s_rows[r - 1], j + 1)
                    sp.dma_start(node_table[b * PT:(b + n) * PT, :].rearrange("(t p) f -> p t f", p=PT),
                                 h_rows[:, b:b + n, :]).then_inc(s_table[r], 16)

            def store_typed(layer, r):
                view = typed_table.rearrange("(b p t) f -> b p (t f)", p=PT, t=T)
                for b in range(NB):
                    sp.wait_ge(s_tab_a[layer], b + 1)
                    sp.wait_ge(s_tab_v[layer], b + 1)
                    sp.dma_start(view[b], table_stage[:, b % 2, :]).then_inc(s_typed_out[r][b % 2], 16)

            store_norm(0, 1)
            store_rows(2)
            store_rows(3)
            store_typed(0, 4)
            store_typed(1, 5)
            store_norm(2, 6)
            store_rows(7)
            store_rows(8)
            store_norm(3, 9)
            for j, (b, n) in enumerate(CHUNKS):
                sp.wait_ge(s_res[3], j + 1)
                sp.dma_start(out[b * PT:(b + n) * PT, :].rearrange("(t p) f -> p t f", p=PT),
                             x_rows[:, b:b + n, :]).then_inc(s_out, 16)
            sp.wait_ge(s_out, 16 * NC)

        @block.gpsimd
        def _(pool):
            pool.iota(node_id[:], pattern=[[1, N]], base=0, channel_multiplier=0,
                      allow_small_or_imprecise_dtypes=True).then_inc(s_ids, 1)
            pool.memset(ident[:], 0.0).then_inc(s_ident, 1)
            pool.wait_ge(s_ident, 1)
            pool.affine_select(out=ident[:], in_=ident[:], compare_op=ALU.not_equal, fill=1.0, base=0,
                               pattern=[[-1, H]], channel_multiplier=1).then_inc(s_ident, 1)
            pool.wait_ge(s_edges, 64)
            copies = pool.alloc_register("ring_copies")
            pool.reg_mov(copies, 1)

            def gather_round(r, table, index):
                at = r * (NG // 2)
                if ROUNDS[r] == TYPED:
                    pool.wait_ge(s_typed_out[r][0], 16 * ((NB + 1) // 2))
                    pool.wait_ge(s_typed_out[r][1], 16 * (NB // 2))
                else:
                    pool.wait_ge(s_table[r], 16 * (1 if r in (1, 6, 9) else NC))
                with pool.Fori(0, NG // 2) as i:
                    for h in range(2):
                        pool.wait_ge(s_free[h], i + (at + 1))
                        lo = h * G
                        pool.tensor_copy(ring[:, lo:lo + G], index[:, bass.ds(i * (2 * G) + lo, G)]).then_inc(s_ring, 1)
                        pool.wait_ge(s_ring, pool.snap(copies, min_val=1))
                        pool.reg_add(copies, copies, 1)
                        for u in range(lo, lo + G):
                            pool.indirect_dma_start(
                                msg[:, u, :], None, table,
                                bass.IndirectOffsetOnAxis(ap=ring[:, u:u + 1], axis=0),
                            ).then_inc(s_gathered[r][h], 16)

            pool.wait_ge(s_typed_idx, 1)
            for r in gather_rounds:
                if ROUNDS[r] == TYPED:
                    gather_round(r, typed_table, typed_i)
                else:
                    gather_round(r, node_table, src_i)

        @block.vector
        def _(dve):
            chain = [0]

            def link(ins):
                chain[0] += 1
                ins.then_inc(s_dve, 1)
                dve.wait_ge(s_dve, chain[0])

            nc.vector.memset(zeros[:], 0.0)
            nc.vector.memset(eps_col[:], EPS)
            nc.vector.memset(ones[:], 1.0).then_inc(s_const, 1)
            dve.wait_ge(s_bounds, 16)
            nc.vector.tensor_reduce(bound_f[:, 0:1], dst_rows[:], AX.X, ALU.min)
            link(nc.vector.tensor_reduce(bound_f[:, 1:2], dst_rows[:], AX.X, ALU.max))
            half = float(PT // 2)
            link(nc.vector.tensor_scalar(bound_f[:, 0:1], bound_f[:, 0:1], -half, 1.0 / PT, ALU.add, ALU.mult))
            link(nc.vector.tensor_scalar(bound_f[:, 1:2], bound_f[:, 1:2], PT - half, 1.0 / PT, ALU.add, ALU.mult))
            nc.vector.tensor_scalar(bound_i[:, 0:1], bound_f[:, 0:1], 0.0, NB - 1.0, ALU.max, ALU.min)
            nc.vector.tensor_scalar(bound_i[:, 1:2], bound_f[:, 1:2], 1.0, float(NB), ALU.max, ALU.min)
            dve.wait_ge(s_edges, 64)
            nc.vector.tensor_copy(dst_f[:], dst_i[:])
            link(nc.vector.tensor_scalar(scaled_src[:], src_i[:], float(T), None, ALU.mult))
            nc.vector.tensor_tensor(typed_i[:], scaled_src[:], typ_i[:], ALU.add).then_inc(s_typed_idx, 1)

            pairs = [dve.alloc_register(f"dve_pairs{h}") for h in range(2)]
            for h in range(2):
                dve.reg_mov(pairs[h], 0)

            def layer_norm(n):
                if n == 0:
                    dve.wait_ge(s_x, 16)
                else:
                    dve.wait_ge(s_res[n - 1], NC)
                for t in range(NB):
                    last = nc.vector.bn_stats(stats[:, t, :], x_rows[:, t, :])
                link(last)
                for t in range(NB):
                    last = nc.vector.bn_aggr(moments[:, t, :], stats[:, t, :])
                last.then_inc(s_var[n], 1)
                dve.wait_ge(s_std[n], 1)
                link(nc.vector.reciprocal(rstd[:], std[:]))
                for t in range(NB):
                    last = nc.vector.tensor_scalar(h_rows[:, t, :], x_rows[:, t, :], moments[:, t, 0:1],
                                                   rstd[:, t:t + 1], ALU.subtract, ALU.mult)
                link(last)
                nc.vector.tensor_scalar(h_rows[:], h_rows[:], 0.0, None, ALU.max).then_inc(s_norm[n], 1)

            def onehots(r):
                with dve.Fori(0, NG // 2) as i:
                    for h in range(2):
                        lo = h * G
                        low = dve.value_load(bounds[0:1, bass.ds(i * 4 + 2 * h, 1)], min_val=0, max_val=NB - 1)
                        high = dve.value_load(bounds[0:1, bass.ds(i * 4 + 2 * h + 1, 1)], min_val=1, max_val=NB)
                        with dve.Fori(low, high) as b:
                            dve.reg_add(pairs[h], pairs[h], 1)
                            dve.wait_ge(s_onehot_used[h], dve.snap(pairs[h], min_val=1))
                            ids = node_id[:, None, bass.ds(b * PT, PT)].to_broadcast([PT, G, PT])
                            mine = dst_f[:, bass.ds(i * (2 * G) + lo, G), None].to_broadcast([PT, G, PT])
                            put = onehot[:, lo:lo + G, :]
                            if ROUNDS[r] != WEIGHTED:
                                nc.vector.tensor_tensor(put, ids, mine, ALU.is_equal).then_inc(s_onehot[h], 1)
                            else:
                                for s in range(G):
                                    k = bass.ds(i * (2 * G) + lo + s, 1)
                                    last = nc.vector.tensor_scalar(
                                        onehot[:, lo + s, :], node_id[:, bass.ds(b * PT, PT)], dst_f[:, k],
                                        weight[:, k], ALU.is_equal, ALU.mult)
                                last.then_inc(s_onehot[h], 1)

            def evacuate(r):
                dve.wait_ge(s_summed[r], 1)
                for j in range(NC):
                    if ROUNDS[r] == SAGE:
                        nc.vector.tensor_tensor(cols3(aggT, j), acc(j), cols3(rdeg, j), ALU.mult).then_inc(s_evac[r], 1)
                    else:
                        nc.vector.tensor_copy(cols3(aggT, j), acc(j)).then_inc(s_evac[r], 1)

            def rows_out(r):
                for j, (b, n) in enumerate(CHUNKS):
                    dve.wait_ge(s_trans[r], j + 1)
                    nc.vector.tensor_copy(h_rows[:, b:b + n, :],
                                          bank(j)[0:PT, 0:n * H].rearrange("p (t f) -> p t f", f=H)).then_inc(s_rows[r], 1)

            def residual(layer):
                for j, (b, n) in enumerate(CHUNKS):
                    dve.wait_ge(s_fin[layer], j + 1)
                    nc.vector.tensor_tensor(x_rows[:, b:b + n, :], x_rows[:, b:b + n, :],
                                            bank(j)[0:PT, 0:n * H].rearrange("p (t f) -> p t f", f=H),
                                            ALU.add).then_inc(s_res[layer], 1)

            def typed_half(layer):
                for b in range(NB):
                    dve.wait_ge(s_tab[layer], b + 1)
                    if b >= 2:
                        dve.wait_ge(s_typed_out[4 + layer][b % 2], 16 * (b // 2))
                    nc.vector.tensor_copy(table_stage[:, b % 2, BANK:2 * BANK],
                                          bank(2 * (b % 4) + 1)[0:PT, :]).then_inc(s_tab_v[layer], 1)

            def gru(layer, r):
                old, new = hT[hT_of[r]], hT[1 - hT_of[r]]

                def first_part(j):
                    q, n = j % 2, CHUNKS[j][1] * PT
                    dve.wait_ge(s_act1[layer], j + 1)
                    link(nc.vector.tensor_tensor(gate_r[:, q, 0:n], gate_r[:, q, 0:n], gate_n[:, q, 0:n], ALU.mult))
                    nc.vector.tensor_tensor(gate_r[:, q, 0:n], gate_r[:, q, 0:n], bank(4 * q + 2)[:, 0:n],
                                            ALU.add).then_inc(s_dve1[layer], 1)

                def second_part(j):
                    q, n = j % 2, CHUNKS[j][1] * PT
                    dve.wait_ge(s_act2[layer], j + 1)
                    link(nc.vector.tensor_tensor(cols(new, j), cols(old, j), gate_n[:, q, 0:n], ALU.subtract))
                    link(nc.vector.tensor_tensor(cols(new, j), cols(new, j), gate_z[:, q, 0:n], ALU.mult))
                    link(nc.vector.tensor_tensor(cols(new, j), cols(new, j), gate_n[:, q, 0:n], ALU.add))
                    nc.vector.tensor_scalar(cols(new, j), cols(new, j), 0.0, None, ALU.max).then_inc(s_new[r], 1)

                for j in range(NC + 1):
                    if j < NC:
                        first_part(j)
                    if j:
                        second_part(j - 1)

            dve.wait_ge(s_weights, 16 * 7)
            nc.vector.tensor_tensor(b_rz[:], b_gru[:, :, 0, 0:2], b_gru[:, :, 1, 0:2], ALU.add).then_inc(s_const, 1)
            layer_norm(0)
            dve.wait_ge(s_ids, 1)
            dve.wait_ge(s_bound_in, 16)
            onehots(0)
            dve.wait_ge(s_summed[0], 1)
            for j in range(NC):
                last = nc.vector.tensor_scalar(cols3(rdeg, j), acc(j), 1.0, None, ALU.max)
                last.then_inc(s_evac[0], 1)
            dve.wait_ge(s_evac[0], NC)
            link(nc.vector.reciprocal(rdeg[:], rdeg[:]))
            for r in (1, 2):
                onehots(r)
                evacuate(r)
                rows_out(r)
            onehots(3)
            evacuate(3)
            residual(0)
            layer_norm(1)
            typed_half(0)
            onehots(4)
            evacuate(4)
            gru(0, 4)
            typed_half(1)
            onehots(5)
            evacuate(5)
            gru(1, 5)
            residual(1)
            layer_norm(2)
            for r in (6, 7):
                onehots(r)
                evacuate(r)
                rows_out(r)
            onehots(8)
            evacuate(8)
            residual(2)
            layer_norm(3)
            onehots(9)
            evacuate(9)
            residual(3)

        @block.tensor
        def _(pe):
            pairs = [pe.alloc_register(f"pe_pairs{h}") for h in range(2)]
            groups = [pe.alloc_register(f"pe_groups{h}") for h in range(2)]
            for h in range(2):
                pe.reg_mov(pairs[h], 0)
            pe.wait_ge(s_const, 2)
            pe.wait_ge(s_ident, 2)
            pe.wait_ge(s_bound_in, 16)
            for h in range(2):
                pe.sem_inc(s_onehot_used[h], 1)
                pe.sem_inc(s_free[h], 1)

            def sum_round(r):
                for h in range(2):
                    pe.reg_mov(groups[h], 1)
                for j in range(NC):
                    nc.tensor.matmul(bank(j), zeros[:, 0:H], zeros[:], start=True, stop=False)
                with pe.Fori(0, NG // 2) as i:
                    for h in range(2):
                        lo = h * G
                        low = pe.value_load(bounds[0:1, bass.ds(i * 4 + 2 * h, 1)], min_val=0, max_val=NB - 1)
                        high = pe.value_load(bounds[0:1, bass.ds(i * 4 + 2 * h + 1, 1)], min_val=1, max_val=NB)
                        if ROUNDS[r] != DEG:
                            pe.wait_ge(s_gathered[r][h], pe.snap(groups[h], min_val=1) * (16 * G))
                            pe.reg_add(groups[h], groups[h], 1)
                        with pe.Fori(low, high) as b:
                            pe.reg_add(pairs[h], pairs[h], 1)
                            pe.wait_ge(s_onehot[h], pe.snap(pairs[h], min_val=1))
                            for s in range(lo, lo + G):
                                what = ones[:] if ROUNDS[r] == DEG else msg[:, s, :]
                                last = nc.tensor.matmul(psum[:, bass.ds(b * H, PT)], what, onehot[:, s, :],
                                                        start=False, stop=False)
                            last.then_inc(s_onehot_used[h], 1)
                        nc.tensor.matmul(spare, zeros[:, 0:1], zeros[:, 0:1], start=True, stop=True).then_inc(s_free[h], 1)
                for j in range(NC):
                    last = nc.tensor.matmul(bank(j), zeros[:, 0:H], zeros[:], start=False, stop=True)
                last.then_inc(s_summed[r], 1)

            def transpose_norm(n):
                pe.wait_ge(s_norm[n], 1)
                for j, (b, m) in enumerate(CHUNKS):
                    for t in range(m):
                        last = nc.tensor.transpose(bank(j)[:, t * PT:(t + 1) * PT], h_rows[:, b + t, :], ident[0:PT, 0:PT])
                    last.then_inc(s_normT[n], 1)

            def sage_mid(r):
                old, new, w = hT[hT_of[r]], hT[1 - hT_of[r]], sage_w[r]
                for j, (b, m) in enumerate(CHUNKS):
                    pe.wait_ge(s_evac[r], j + 1)
                    o = bank(j)[:, 0:m * PT]
                    nc.tensor.matmul(o, w_sage[:, w, :], cols(aggT, j), start=True, stop=False)
                    nc.tensor.matmul(o, w_sage[:, w + 1, :], cols(old, j), start=False, stop=True).then_inc(s_lin[r], 1)
                for j, (b, m) in enumerate(CHUNKS):
                    pe.wait_ge(s_new[r], j + 1)
                    for t in range(m):
                        last = nc.tensor.transpose(bank(j)[0:PT, t * H:(t + 1) * H],
                                                   new[:, (b + t) * PT:(b + t + 1) * PT], ident[:])
                    last.then_inc(s_trans[r], 1)

            def final_rows(layer, ready, terms, bias):
                ready()
                for j, (b, m) in enumerate(CHUNKS):
                    for t in range(m):
                        o = bank(j)[0:PT, t * H:(t + 1) * H]
                        for n, (x, w) in enumerate(terms):
                            last = nc.tensor.matmul(o, x[:, (b + t) * PT:(b + t + 1) * PT], w, start=n == 0,
                                                    stop=bias is None and n == len(terms) - 1)
                        if bias is not None:
                            last = nc.tensor.matmul(o, ones[0:1, 0:PT], bias, start=False, stop=True)
                    last.then_inc(s_fin[layer], 1)

            def typed_products(layer, cur, ready):
                ready()
                for b in range(NB):
                    if b >= 4:
                        pe.wait_ge(s_tab_a[layer], b - 3)
                        pe.wait_ge(s_tab_v[layer], b - 3)
                    for q in range(2):
                        last = nc.tensor.matmul(bank(2 * (b % 4) + q)[0:PT, :], cur[:, b * PT:(b + 1) * PT],
                                                w_typed[:, (2 * layer + q) * BANK:(2 * layer + q + 1) * BANK],
                                                start=True, stop=True)
                    last.then_inc(s_tab[layer], 1)

            def gru(layer, r):
                old = hT[hT_of[r]]
                pe.wait_ge(s_evac[r], NC)
                for j, (b, m) in enumerate(CHUNKS):
                    q, n = j % 2, m * PT
                    if j >= 2:
                        pe.wait_ge(s_dve1[layer], j - 1)
                    for g in range(2):
                        o = bank(4 * q + g)[:, 0:n]
                        nc.tensor.matmul(o, w_gru[:, layer, 0, g * H:(g + 1) * H], cols(aggT, j), start=True, stop=False)
                        nc.tensor.matmul(o, w_gru[:, layer, 1, g * H:(g + 1) * H], cols(old, j), start=False, stop=True)
                    nc.tensor.matmul(bank(4 * q + 2)[:, 0:n], w_gru[:, layer, 0, 2 * H:3 * H], cols(aggT, j), start=True, stop=True)
                    nc.tensor.matmul(bank(4 * q + 3)[:, 0:n], w_gru[:, layer, 1, 2 * H:3 * H], cols(old, j),
                                     start=True, stop=True).then_inc(s_lin[r], 1)

            sum_round(0)
            pe.wait_ge(s_evac[0], NC)
            transpose_norm(0)
            pe.wait_ge(s_normed[0], NC)
            sum_round(1)
            sage_mid(1)
            pe.wait_ge(s_rows[1], NC)
            sum_round(2)
            sage_mid(2)
            pe.wait_ge(s_rows[2], NC)
            sum_round(3)
            final_rows(0, lambda: pe.wait_ge(s_evac[3], NC),
                       [(aggT, w_sage[:, 4, :]), (hT[0], w_sage[:, 5, :])], b_row[:, 0:H])
            pe.wait_ge(s_res[0], NC)
            transpose_norm(1)
            for j, (b, m) in enumerate(CHUNKS):
                pe.wait_ge(s_normed[1], j + 1)
                nc.tensor.matmul(bank(j)[:, 0:m * PT], w_misc[:, 0, :], cols(hT[0], j), start=True, stop=True).then_inc(s_proj, 1)
            typed_products(0, hT[1], lambda: pe.wait_ge(s_projed, NC))
            pe.wait_ge(s_tab_a[0], NB)
            pe.wait_ge(s_tab_v[0], NB)
            sum_round(4)
            gru(0, 4)
            typed_products(1, hT[0], lambda: pe.wait_ge(s_new[4], NC))
            pe.wait_ge(s_tab_a[1], NB)
            pe.wait_ge(s_tab_v[1], NB)
            sum_round(5)
            gru(1, 5)
            final_rows(1, lambda: pe.wait_ge(s_new[5], NC), [(hT[1], w_misc[:, 1, :])], b_row[:, 2 * H:3 * H])
            pe.wait_ge(s_res[1], NC)
            transpose_norm(2)
            pe.wait_ge(s_normed[2], NC)
            sum_round(6)
            sage_mid(6)
            pe.wait_ge(s_rows[6], NC)
            sum_round(7)
            sage_mid(7)
            pe.wait_ge(s_rows[7], NC)
            sum_round(8)
            final_rows(2, lambda: pe.wait_ge(s_evac[8], NC),
                       [(aggT, w_sage[:, 10, :]), (hT[0], w_sage[:, 11, :])], b_row[:, H:2 * H])
            pe.wait_ge(s_res[2], NC)
            sum_round(9)
            final_rows(3, lambda: pe.wait_ge(s_evac[9], NC), [(aggT, w_misc[:, 2, :])], None)

        @block.scalar
        def _(act):
            for dst, src in ((w_sage, "w_sage"), (b_col, "b_col"), (b_row, "b_row"), (w_typed, "w_typed"),
                             (w_gru, "w_gru"), (b_gru, "b_gru"), (w_misc, "w_misc")):
                act.dma_start(dst[:], a[src]).then_inc(s_weights, 16)

            def root(n):
                act.wait_ge(s_var[n], 1)
                nc.scalar.activation(std[:], moments[:, :, 1], ACT.Sqrt, bias=eps_col[:]).then_inc(s_std[n], 1)

            def norm_out(n):
                for j, (b, m) in enumerate(CHUNKS):
                    act.wait_ge(s_normT[n], j + 1)
                    nc.scalar.activation(cols(hT[0], j), bank(j)[:, 0:m * PT], ACT.Copy).then_inc(s_normed[n], 1)

            def sage_mid(r):
                new = hT[1 - hT_of[r]]
                for j, (b, m) in enumerate(CHUNKS):
                    act.wait_ge(s_lin[r], j + 1)
                    nc.scalar.activation(cols(new, j), bank(j)[:, 0:m * PT], ACT.Relu,
                                         bias=b_col[:, bias_col[r]:bias_col[r] + 1]).then_inc(s_new[r], 1)

            def typed_half(layer):
                for b in range(NB):
                    act.wait_ge(s_tab[layer], b + 1)
                    if b >= 2:
                        act.wait_ge(s_typed_out[4 + layer][b % 2], 16 * (b // 2))
                    nc.scalar.activation(table_stage[:, b % 2, 0:BANK], bank(2 * (b % 4))[0:PT, :],
                                         ACT.Copy).then_inc(s_tab_a[layer], 1)

            def gru(layer, r):
                def gates(j):
                    q, n = j % 2, CHUNKS[j][1] * PT
                    act.wait_ge(s_lin[r], j + 1)
                    if j >= 2:
                        act.wait_ge(s_new[r], j - 1)
                    nc.scalar.activation(gate_r[:, q, 0:n], bank(4 * q)[:, 0:n], ACT.Sigmoid, bias=b_rz[:, layer, 0:1])
                    nc.scalar.activation(gate_z[:, q, 0:n], bank(4 * q + 1)[:, 0:n], ACT.Sigmoid, bias=b_rz[:, layer, 1:2])
                    nc.scalar.activation(gate_n[:, q, 0:n], bank(4 * q + 3)[:, 0:n], ACT.Identity,
                                         bias=b_gru[:, layer, 1, 2:3]).then_inc(s_act1[layer], 1)

                def candidate(j):
                    q, n = j % 2, CHUNKS[j][1] * PT
                    act.wait_ge(s_dve1[layer], j + 1)
                    nc.scalar.activation(gate_n[:, q, 0:n], gate_r[:, q, 0:n], ACT.Tanh,
                                         bias=b_gru[:, layer, 0, 2:3]).then_inc(s_act2[layer], 1)

                for j in range(NC + 1):
                    if j < NC:
                        gates(j)
                    if j:
                        candidate(j - 1)

            act.wait_ge(s_const, 2)
            root(0)
            norm_out(0)
            sage_mid(1)
            sage_mid(2)
            root(1)
            norm_out(1)
            for j, (b, m) in enumerate(CHUNKS):
                act.wait_ge(s_proj, j + 1)
                nc.scalar.activation(cols(hT[1], j), bank(j)[:, 0:m * PT], ACT.Relu, bias=b_col[:, 4:5]).then_inc(s_projed, 1)
            typed_half(0)
            gru(0, 4)
            typed_half(1)
            gru(1, 5)
            root(2)
            norm_out(2)
            sage_mid(6)
            sage_mid(7)
            root(3)


def laid_out(i):
    import numpy as np

    def tiles(v):
        return np.ascontiguousarray(np.asarray(v).reshape(NTILE, PT).T)

    def t(v):
        return np.asarray(v).T

    i = {k: np.asarray(v) for k, v in i.items()}
    sage = [t(i["L0_gnn_Wl0"]), t(i["L0_gnn_Wr0"]), t(i["L0_gnn_Wl1"]), t(i["L0_gnn_Wr1"]), t(i["L0_gnn_Wl2"]), t(i["L0_gnn_Wr2"])]
    for n in range(3):
        sage += [i["L2_gnn_Wl"][n], i["L2_gnn_Wr"][n]]
    gru = np.stack([i["L1_gnn_gru_wih"], i["L1_gnn_gru_whh"]])
    gru_b = np.stack([i["L1_gnn_gru_bih"], i["L1_gnn_gru_bhh"]])
    put = {
        "dst_rows": i["dst"].reshape(NG, G * PT), "dst_t": tiles(i["dst"]), "src_t": tiles(i["src"]),
        "typ_t": tiles(i["edge_type_8"]), "weight_t": tiles(i["edge_weight"]), "x": i["x"],
        "w_sage": np.stack(sage, 1),
        "b_col": np.stack([i["L0_gnn_bl0"], i["L0_gnn_bl1"], i["L2_gnn_b"][0], i["L2_gnn_b"][1], i["L1_gnn_node_proj_b"]], 1),
        "b_row": np.concatenate([i["L0_gnn_bl2"], i["L2_gnn_b"][2], i["L1_gnn_out_b"]])[None],
        "w_typed": i["L1_gnn_edge_W"].transpose(3, 0, 1, 2).reshape(H, 2 * T * H),
        "w_gru": gru.transpose(3, 1, 0, 2),
        "b_gru": gru_b.reshape(2, 2, 3, H).transpose(3, 1, 0, 2),
        "w_misc": np.stack([t(i["L1_gnn_node_proj_w"]), t(i["L1_gnn_out_w"]), t(i["L3_gnn_W"])], 1),
    }
    return {k: np.ascontiguousarray(v) for k, v in put.items()}


def kernel(**inputs):
    import concourse.bacc as bacc
    from concourse.bass_utils import run_bass_kernel_spmd

    arrays = laid_out(inputs)
    nc = bacc.Bacc("TRN2", target_bir_lowering=False, num_devices=1)
    aps = {k: nc.dram_tensor(f"in_{k}", v.shape, mybir.dt.from_np(v.dtype), kind="ExternalInput").ap()
           for k, v in arrays.items()}
    out = nc.dram_tensor("out_x", (N, H), F32, kind="ExternalOutput").ap()
    gnn_program(nc, aps, out)
    got = run_bass_kernel_spmd(nc, [{f"in_{k}": v for k, v in arrays.items()}], core_ids=[0])
    return got.results[0]["out_x"]
```

```python
from contextlib import ExitStack

import concourse.bass as bass
from concourse import mybir

F32 = mybir.dt.float32
F16 = mybir.dt.float16
BF16 = mybir.dt.bfloat16
I32 = mybir.dt.int32
U32 = mybir.dt.uint32
ALU = mybir.AluOpType
ACT = mybir.ActivationFunctionType
AX = mybir.AxisListType

N, E, H, T = 3125, 100000, 128, 8
PT = 125
NB = N // PT
NTILE = E // PT
G = 8
NG = NTILE // G
U = 2
NU = NTILE // U
WN = 20
NW = (N + WN - 1) // WN
KEYS = WN * NB
RING = 4
PACK = 1024
PACK_BITS = PACK.bit_length() - 1
EPS = 1e-5
BANK = 512
CHUNKS = [(4 * j, min(4, NB - 4 * j)) for j in range((NB + 3) // 4)]
NC = len(CHUNKS)
ORDER = [NC - 1] + list(range(NC - 1))
HALVES = [(2 * c, min(2, NB - 2 * c)) for c in range((NB + 1) // 2)]

SAGE, TYPED, WEIGHTED = "sage", "typed", "weighted"
ROUNDS = [SAGE, SAGE, SAGE, TYPED, TYPED, SAGE, SAGE, SAGE, WEIGHTED]
FINAL_ROUND = [2, 4, 7, 8]
SPREADS = ["N0", "M0", "M1", "N1", "N2", "M5", "M6", "N3"]
STORED = ["N0", "M0", "M1", "N2", "M5", "M6", "N3"]
SPLIT = ["N0", "M0", "M1", "N2", "M5", "M6"]
TURNED = [x for x in SPREADS if x != "N3"]


def gnn_program(nc, a, out):
    ctx = ExitStack()
    with ctx:
        def sb(name, shape, dt=F32):
            return ctx.enter_context(nc.sbuf_tensor(name, shape, dt))

        def sem(name):
            return ctx.enter_context(nc.semaphore(name))

        def two(name):
            return [sem(f"{name}{q}") for q in range(2)]

        def dram(name, shape, dt=F32):
            return nc.dram_tensor(name, shape, dt).ap()

        node_table = dram("node_table", (N, H))
        typed_table = dram("typed_table", (N * T, H))
        x_dram = dram("x_dram", (N, H))
        typed_index = dram("typed_index", (PT, NTILE), I32)
        group_scratch = dram("group_scratch", (NG, 1), I32)
        unit_scratch = dram("unit_scratch", (2, NU))
        window_scratch = dram("window_scratch", (2 * H, 1), I32)

        counts = sb("counts", [PT, NB, N], BF16)
        dst_f = sb("dst_f", [PT, NTILE])
        group_bounds = sb("group_bounds", [1, NG], I32)
        w_layer = sb("w_layer", [H, 6 * H])
        w_single = sb("w_single", [H, H])
        b_rows = sb("b_rows", [3 * 32, H])
        b_proj = sb("b_proj", [H, 1])
        b_gru = sb("b_gru", [H, 2, 2, 3])
        b_rz = sb("b_rz", [H, 2, 2])
        ident = sb("ident", [H, H])
        ones = sb("ones", [PT, H])
        zeros = sb("zeros", [1, H], BF16)
        block_ids = sb("block_ids", [PT, PT])
        block_base = sb("block_base", [PT, NB])
        rdeg = sb("rdeg", [PT, NB])
        moments = sb("moments", [PT, NB, 2])
        std = sb("std", [PT, NB])
        rstd = sb("rstd", [PT, NB])
        eps_col = sb("eps_col", [PT, 1])
        over_col = sb("over_col", [PT, 1])
        over_flag = sb("over_flag", [1, 1], I32)
        WORK_R, WORK_ROWS, WORK_AGG, WORK_TMP, WORK_U = NB * H, 2 * BANK, 2 * BANK, 2 * BANK, 5120
        work = sb("work", [H, WORK_R + WORK_ROWS + WORK_AGG + WORK_TMP + WORK_U])
        at = [0]

        def carve(size):
            at[0] += size
            return work[:, at[0] - size:at[0]]

        def blocks(v, dt=F32):
            return v.rearrange("p (b c) -> p b c", c=H)

        region = blocks(carve(WORK_R))
        rows = carve(WORK_ROWS).rearrange("p (q c) -> p q c", q=2)
        agg = carve(WORK_AGG).rearrange("p (q c) -> p q c", q=2)
        tmp = carve(WORK_TMP).rearrange("p (q c) -> p q c", q=2)
        union = carve(WORK_U)
        x_rows = region[0:PT]
        hT = region
        w_types = work[:, WORK_R + WORK_ROWS:WORK_R + WORK_ROWS + T * H]
        stats = tmp[0:PT, 0, 0:NB * 6].rearrange("p (b s) -> p b s", s=6)
        parts = union[0:PT, 0:3 * NB * H // 2].bitcast(BF16).rearrange("p (k b f) -> p k b f", k=3, f=H)
        msg = union[0:PT, 0:2 * G * H].rearrange("p (s f) -> p s f", f=H)
        onehot = union[0:PT, 2048:2048 + 2 * G * PT].rearrange("p (s c) -> p s c", c=PT)
        index = union[0:PT, 4096:4096 + NTILE].bitcast(I32)
        ring = union[0:PT, 4096 + NTILE:4096 + NTILE + 2 * G].bitcast(U32)
        weight = region[0:PT].rearrange("p b c -> p (b c)")[:, 0:NTILE]
        table_stage = union[0:PT, 0:2 * T * H].rearrange("p (q c) -> p q c", q=2)
        aggT = union[:, 0:N].rearrange("p (b c) -> p b c", c=PT)
        gates = union[:, 3200:3200 + 6 * 2 * PT].rearrange("p (g q c) -> p g q c", g=3, q=2)
        gate_r, gate_z, gate_n = gates[:, 0], gates[:, 1], gates[:, 2]
        at[0] = 0
        dst_i = carve(NTILE)[0:PT].bitcast(I32)
        src_i = carve(NTILE)[0:PT].bitcast(I32)
        typ_i = carve(NTILE)[0:PT].bitcast(I32)
        dst_nat = carve(G * PT)[0:NG].bitcast(I32).rearrange("g (u e) -> g u e", e=U * PT)
        hi_f = carve(NTILE)[0:PT]
        lo_wide = carve(NTILE + U)[0:PT]
        key_wide = carve(NTILE + U)[0:PT]
        lo_f, key_f = lo_wide[:, 0:NTILE], key_wide[:, 0:NTILE]
        typed_i = carve(NTILE)[0:PT].bitcast(I32)
        unit_lo = carve(NU)
        unit_hi = carve(NU)
        unit_up = carve(NU)
        unit_down = carve(NU)
        deg_row = work[0:1, at[0] - 4 * NU:at[0] - 4 * NU + 2 * BANK].rearrange("p (q c) -> p q c", q=2)
        lies = [carve(NU) for _ in range(2)]
        met = [carve(NU) for _ in range(2)]
        hi_i = work[0:PT, at[0] - 2 * NU:at[0]].bitcast(I32)
        window_id = carve(2)
        window_f = carve(4).rearrange("p (h c) -> p h c", c=2)
        window_i = carve(2).bitcast(I32)
        unit_f = carve(2 * U * 2)[0:NG].rearrange("g (c u) -> g c u", c=2)
        group_f = carve(2)[0:NG]
        group_b = carve(2)[0:NG].bitcast(I32)
        group_i = carve(1)[0:NG].bitcast(I32)
        window_base = carve(NW)[0:PT]
        window_bounds = carve(2 * H)[0:1].bitcast(I32)
        key_ids = carve(KEYS // 2)[0:PT].bitcast(F16)
        lo_ids = carve(64)[0:PT].bitcast(F16)[:, 0:PT]
        key_size, lo_size = RING * U * KEYS // 2, RING * U * H // 2
        assert NU * 2 == NTILE and key_size + lo_size <= 3 * NTILE + G * PT
        key_hot = work[0:PT, 0:key_size].bitcast(BF16)
        lo_hot = work[0:PT, key_size:key_size + lo_size].bitcast(BF16)
        zero_keys = carve(KEYS // 2)[0:1].bitcast(BF16)
        over_parts = carve(NW)[0:PT]
        ones_bf = carve(H // 2)[0:PT].bitcast(BF16)
        assert at[0] <= WORK_R + 3 * 2 * BANK + WORK_U, at[0]

        psum = ctx.enter_context(nc.psum_tensor("psum", [H, 8 * BANK], F32))

        def bank(j):
            return psum[:, j * BANK:(j + 1) * BANK]

        def acc(j):
            n = CHUNKS[j][1]
            return bank(j)[:, 0:n * H].rearrange("p (b c) -> p b c", c=H)[:, :, 0:PT]

        def root_bank(i):
            return bank(7 if i % 2 == 0 else NC - 1)

        def turned_bank(i):
            return bank(7 if i == 0 else ORDER[i])

        spare = bank(7)[0:1, BANK - 1:BANK]

        s_dst, s_edges, s_x, s_proj_in = sem("s_dst"), sem("s_edges"), sem("s_x"), sem("s_proj_in")
        s_small = sem("s_small")
        s_layer_w = [sem(f"s_layer_w{n}") for n in range(4)]
        s_single_w = [sem(f"s_single_w{n}") for n in range(3)]
        s_types_w = two("s_types_w")
        s_const, s_ids, s_ident = sem("s_const"), sem("s_ids"), sem("s_ident")
        s_dve, s_pool = sem("s_dve"), sem("s_pool")
        s_unit_f, s_group_i, s_window_i, s_typed = sem("s_unit_f"), sem("s_group_i"), sem("s_window_i"), sem("s_typed")
        s_scratch_out = [sem(f"s_scratch_out{n}") for n in range(3)]
        s_scratch_in = [sem(f"s_scratch_in{n}") for n in range(3)]
        s_typed_out = sem("s_typed_out")
        s_unit, s_unit_used = sem("s_unit"), sem("s_unit_used")
        s_window, s_counted, s_bank_free = sem("s_window"), sem("s_counted"), two("s_bank_free")
        s_raw = sem("s_raw")
        s_over_sum, s_over = sem("s_over_sum"), sem("s_over")
        s_deg, s_deg_row, s_deg_turned, s_rdeg = sem("s_deg"), sem("s_deg_row"), sem("s_deg_turned"), sem("s_rdeg")
        s_index = [sem(f"s_index{r}") for r in range(len(ROUNDS))]
        s_ring = sem("s_ring")
        s_free, s_onehot, s_onehot_used, s_gathered = two("s_free"), two("s_onehot"), two("s_onehot_used"), two("s_gathered")
        s_summed = sem("s_summed")
        s_evac = sem("s_evac")
        s_lin = sem("s_lin")
        s_pre, s_h, s_r1, s_p2, s_p3 = sem("s_pre"), sem("s_h"), sem("s_r1"), sem("s_p2"), sem("s_p3")
        s_root = sem("s_root")
        s_trans, s_turned = sem("s_trans"), sem("s_turned")
        s_stored = two("s_stored")
        s_std_in, s_std = sem("s_std_in"), sem("s_std")
        s_resid = sem("s_resid")
        s_x_old = two("s_x_old")
        s_x_out = [sem(f"s_x_out{n}") for n in range(4)]
        s_proj, s_projed = sem("s_proj"), sem("s_projed")
        s_tab, s_tab_a, s_tab_v = sem("s_tab"), sem("s_tab_a"), sem("s_tab_v")
        s_staged = two("s_staged")
        s_agg_a, s_agg_v = sem("s_agg_a"), sem("s_agg_v")
        s_gates, s_act1, s_dve1, s_act2, s_gru = sem("s_gates"), sem("s_act1"), sem("s_dve1"), sem("s_act2"), sem("s_gru")

        block = ctx.enter_context(nc.Block())

        def spread_at(stage):
            return NC * SPREADS.index(stage)

        def before(stage, kinds):
            return NC * sum(x in kinds for x in SPREADS[:SPREADS.index(stage)])

        def stores_before(stage, q):
            n = 0
            for x in SPREADS[:SPREADS.index(stage)]:
                n += sum(x in STORED and (spread_at(x) + i) % 2 == q for i in range(NC))
            return n

        LIN_ROUNDS = ["M0", "M1", "F0", "F1", "M5", "M6", "F2", "F3"]
        EVAC_ROUNDS = [x for x in LIN_ROUNDS if x != "F1"]

        ROOTS = ["M0", "M1", "F0", "M5", "M6", "F2"]

        def lin_at(stage):
            return NC * LIN_ROUNDS.index(stage)

        def evac_at(stage):
            return NC * EVAC_ROUNDS.index(stage)

        def buffer_free(eng, c):
            if c >= 2:
                eng.wait_ge(s_h, c - 1)
                turned = sum(x in TURNED for x in SPREADS[:(c - 2) // NC])
                if SPREADS[(c - 2) // NC] in TURNED:
                    eng.wait_ge(s_trans, NC * turned + (c - 2) % NC + 1)
                split = sum(x in SPLIT for x in SPREADS[:(c - 2) // NC])
                if SPREADS[(c - 2) // NC] in SPLIT:
                    eng.wait_ge(s_r1, NC * split + (c - 2) % NC + 1)
                stored = sum(x % 2 == c % 2 and SPREADS[x // NC] in STORED for x in range(c - 1))
                eng.wait_ge(s_stored[c % 2], 16 * stored)

        def chunk_rows(dram_rows, j):
            b, n = CHUNKS[j]
            return dram_rows[b * PT:(b + n) * PT, :].rearrange("(t p) f -> p t f", p=PT)

        def load_range(eng, bounds, at, most, pair):
            both = eng.value_load(bounds[0:1, bass.ds(at, 1)], min_val=1, max_val=PACK * most)
            low, high = pair
            eng.reg_alu(low, both, PACK_BITS, ALU.logical_shift_right)
            eng.reg_alu(high, both, PACK - 1, ALU.bitwise_and)
            return eng.snap(low, min_val=0, max_val=most - 1), eng.snap(high, min_val=1, max_val=most)

        @block.sync
        def _(sp):
            sp.dma_start(dst_nat, a["dst_rows"].rearrange("g (u e) -> g u e", e=U * PT)).then_inc(s_dst, 16)
            sp.dma_start(src_i, a["src_t"]).then_inc(s_edges, 16)
            sp.dma_start(dst_i, a["dst_t"]).then_inc(s_edges, 16)
            sp.dma_start(typ_i, a["typ_t"]).then_inc(s_edges, 16)
            sp.wait_ge(s_unit_f, 1)
            for c in range(2):
                sp.dma_start(unit_scratch[c].rearrange("(g u) -> g u", g=NG), unit_f[:, c, :]).then_inc(s_scratch_out[0], 16)
            sp.wait_ge(s_scratch_out[0], 32)
            sp.dma_start(unit_lo, unit_scratch[0:1, :].to_broadcast([H, NU])).then_inc(s_scratch_in[0], 16)
            sp.dma_start(unit_hi, unit_scratch[1:2, :].to_broadcast([H, NU])).then_inc(s_scratch_in[0], 16)
            sp.wait_ge(s_group_i, 1)
            sp.dma_start(group_scratch, group_i).then_inc(s_scratch_out[1], 16)
            sp.wait_ge(s_window_i, 1)
            for h in range(2):
                sp.dma_start(window_scratch[h * H:(h + 1) * H, :], window_i[:, h:h + 1]).then_inc(s_scratch_out[2], 16)
            sp.wait_ge(s_scratch_out[2], 32)
            sp.dma_start(window_bounds, window_scratch.rearrange("(a w) c -> a (w c)", a=1)).then_inc(s_scratch_in[2], 16)
            sp.wait_ge(s_scratch_out[1], 16)
            sp.dma_start(group_bounds[:], group_scratch.rearrange("(a g) c -> a (g c)", a=1)).then_inc(s_scratch_in[1], 16)
            sp.wait_ge(s_typed, 1)
            sp.dma_start(typed_index, typed_i).then_inc(s_typed_out, 16)
            sp.wait_ge(s_typed_out, 16)

            def load_index(r, src):
                sp.dma_start(index, src).then_inc(s_index[r], 16)

            def store_spread(stage):
                for i, j in enumerate(ORDER):
                    c = spread_at(stage) + i
                    sp.wait_ge(s_h, c + 1)
                    n = CHUNKS[j][1]
                    sp.dma_start(chunk_rows(node_table, j),
                                 rows[0:PT, c % 2, 0:n * H].rearrange("p (t f) -> p t f", f=H)).then_inc(s_stored[c % 2], 16)

            def sage_index(r, stage):
                over = sp.value_load(over_flag[0:1, 0:1], min_val=0, max_val=1)
                with sp.If(over > 0):
                    sp.wait_ge(s_p3, before(stage, SPLIT) + NC)
                    load_index(r, a["src_t"])
                with sp.Else():
                    sp.nop()

            def final(n, r):
                for i in range(NC + 2):
                    if i < NC:
                        j, c = ORDER[i], NC * n + i
                        if i >= 2:
                            sp.wait_ge(s_resid, c - 1)
                        m = CHUNKS[j][1]
                        x_from = a["x"] if n == 0 else x_dram
                        if i == 0 and n == 0:
                            sp.wait_ge(s_p3, before("M1", SPLIT) + NC)
                        if i == 0 and n == 2:
                            sp.wait_ge(s_p3, before("M6", SPLIT) + NC)
                        if i == 0 and n == 1:
                            sp.wait_ge(s_r1, 0 + before("N1", SPLIT))
                        sp.dma_start(tmp[0:PT, c % 2, 0:m * H].rearrange("p (t f) -> p t f", f=H),
                                     chunk_rows(x_from, j)).then_inc(s_x_old[c % 2], 16)
                    if i >= 2:
                        j, c = ORDER[i - 2], NC * n + i - 2
                        b, m = CHUNKS[j]
                        sp.wait_ge(s_resid, c + 1)
                        sp.dma_start(chunk_rows(out if n == 3 else x_dram, j), x_rows[:, b:b + m, :]).then_inc(s_x_out[n], 16)

            def store_typed(layer):
                view = typed_table.rearrange("(b p t) f -> b p (t f)", p=PT, t=T)
                for b in range(NB):
                    c = NB * layer + b
                    sp.wait_ge(s_tab_a, c + 1)
                    sp.wait_ge(s_tab_v, c + 1)
                    sp.dma_start(view[b], table_stage[:, c % 2, :]).then_inc(s_staged[c % 2], 16)

            sp.wait_ge(s_rdeg, 1)
            sp.dma_start(x_rows, a["x"].rearrange("(t p) f -> p t f", p=PT)).then_inc(s_x, 16)
            store_spread("N0")
            sage_index(0, "N0")
            store_spread("M0")
            sage_index(1, "M0")
            store_spread("M1")
            sage_index(2, "M1")
            final(0, 2)
            sp.wait_ge(s_lin, lin_at("F0") + NC)
            sp.dma_start(w_layer[:], a["w_gru0"]).then_inc(s_layer_w[1], 16)
            sp.dma_start(b_rows[0:1, :], a["b_out"]).then_inc(s_layer_w[1], 16)
            sp.dma_start(w_types, a["w_types0"]).then_inc(s_types_w[0], 16)
            sp.wait_ge(s_proj, NC)
            sp.dma_start(w_single[:], a["w_out"]).then_inc(s_single_w[1], 16)
            sp.wait_ge(s_over, 1)
            load_index(3, typed_index)
            store_typed(0)
            sp.wait_ge(s_tab, NB)
            sp.dma_start(w_types, a["w_types1"]).then_inc(s_types_w[1], 16)
            sp.wait_ge(s_gates, len(HALVES))
            sp.dma_start(w_layer[:], a["w_gru1"]).then_inc(s_layer_w[2], 16)
            sp.wait_ge(s_gru, len(HALVES))
            load_index(4, typed_index)
            store_typed(1)
            sp.wait_ge(s_gates, 2 * len(HALVES))
            sp.dma_start(w_layer[:], a["w_sage2"]).then_inc(s_layer_w[3], 16)
            final(1, 4)
            sp.wait_ge(s_lin, lin_at("F1") + NC)
            for n in range(3):
                sp.dma_start(b_rows[32 * n:32 * n + 1, :], a["b_sage2"][n:n + 1, :]).then_inc(s_layer_w[3], 16)
            sp.dma_start(w_single[:], a["w_last"]).then_inc(s_single_w[2], 16)
            store_spread("N2")
            sage_index(5, "N2")
            store_spread("M5")
            sage_index(6, "M5")
            store_spread("M6")
            sage_index(7, "M6")
            final(2, 7)
            load_index(8, a["src_t"])
            store_spread("N3")
            sp.wait_ge(s_pre, spread_at("N3") + NC)
            sp.wait_ge(s_x_out[2], 16 * NC)
            sp.dma_start(weight, a["weight_t"]).then_inc(s_index[8], 16)
            sp.wait_ge(s_summed, 9)
            final(3, 8)
            sp.wait_ge(s_x_out[3], 16 * NC)

        @block.gpsimd
        def _(pool):
            pool.iota(key_ids, pattern=[[1, KEYS]], base=0, channel_multiplier=0,
                      allow_small_or_imprecise_dtypes=True).then_inc(s_ids, 1)
            pool.iota(block_ids[:], pattern=[[1, PT]], base=0, channel_multiplier=0,
                      allow_small_or_imprecise_dtypes=True).then_inc(s_ids, 1)
            pool.iota(block_base[:], pattern=[[PT, NB]], base=0, channel_multiplier=0,
                      allow_small_or_imprecise_dtypes=True).then_inc(s_ids, 1)
            pool.iota(window_base, pattern=[[KEYS, NW]], base=0, channel_multiplier=0,
                      allow_small_or_imprecise_dtypes=True).then_inc(s_ids, 1)
            pool.iota(window_id, pattern=[[H, 2]], base=0, channel_multiplier=1,
                      allow_small_or_imprecise_dtypes=True).then_inc(s_ids, 1)
            pool.iota(unit_up, pattern=[[1, NU]], base=1, channel_multiplier=0,
                      allow_small_or_imprecise_dtypes=True).then_inc(s_ids, 1)
            pool.iota(unit_down, pattern=[[-1, NU]], base=NU, channel_multiplier=0,
                      allow_small_or_imprecise_dtypes=True).then_inc(s_ids, 1)
            pool.iota(lo_ids, pattern=[[1, PT]], base=0, channel_multiplier=0,
                      allow_small_or_imprecise_dtypes=True).then_inc(s_ids, 1)
            pool.memset(ident[:], 0.0).then_inc(s_pool, 1)
            pool.wait_ge(s_pool, 1)
            pool.affine_select(out=ident[:], in_=ident[:], compare_op=ALU.not_equal, fill=1.0, base=0,
                               pattern=[[-1, H]], channel_multiplier=1).then_inc(s_ident, 1)
            copies = pool.alloc_register("ring_copies")
            pool.reg_mov(copies, 1)
            free = [pool.alloc_register(f"groups_freed{h}") for h in range(2)]
            for h in range(2):
                pool.reg_mov(free[h], 1)

            def gather(r, table):
                pool.wait_ge(s_index[r], 32 if ROUNDS[r] == WEIGHTED else 16)
                with pool.Fori(0, NG // 2) as i:
                    for h in range(2):
                        pool.wait_ge(s_free[h], pool.snap(free[h], min_val=1))
                        pool.reg_add(free[h], free[h], 1)
                        lo = h * G
                        pool.tensor_copy(ring[:, lo:lo + G], index[:, bass.ds(i * (2 * G) + lo, G)]).then_inc(s_ring, 1)
                        pool.wait_ge(s_ring, pool.snap(copies, min_val=1))
                        pool.reg_add(copies, copies, 1)
                        for u in range(lo, lo + G):
                            pool.indirect_dma_start(
                                msg[:, u, :], None, table,
                                bass.IndirectOffsetOnAxis(ap=ring[:, u:u + 1], axis=0),
                            ).then_inc(s_gathered[h], 16)

            def rows_in_table(stage):
                for q in range(2):
                    mine = sum((spread_at(stage) + i) % 2 == q for i in range(NC))
                    pool.wait_ge(s_stored[q], 16 * (stores_before(stage, q) + mine))

            def sage(r, stage):
                over = pool.value_load(over_flag[0:1, 0:1], min_val=0, max_val=1)
                with pool.If(over > 0):
                    rows_in_table(stage)
                    gather(r, node_table)
                with pool.Else():
                    pool.nop()

            pool.wait_ge(s_over, 1)
            sage(0, "N0")
            sage(1, "M0")
            sage(2, "M1")
            for layer in range(2):
                for q in range(2):
                    done = sum(c % 2 == q for c in range(NB * (layer + 1)))
                    pool.wait_ge(s_staged[q], 16 * done)
                gather(3 + layer, typed_table)
            sage(5, "N2")
            sage(6, "M5")
            sage(7, "M6")
            rows_in_table("N3")
            gather(8, node_table)

        @block.vector
        def _(dve):
            chain = [0]

            def link(ins):
                chain[0] += 1
                ins.then_inc(s_dve, 1)
                dve.wait_ge(s_dve, chain[0])

            v = nc.vector
            v.memset(zeros[:], 0.0)
            v.memset(zero_keys, 0.0)
            v.memset(eps_col[:], EPS)
            v.memset(over_col[:], -255.0)
            v.memset(ones_bf, 1.0)
            v.memset(ones[:], 1.0).then_inc(s_const, 1)

            dve.wait_ge(s_dst, 16)
            v.tensor_reduce(unit_f[:, 0, :], dst_nat, AX.X, ALU.min)
            link(v.tensor_reduce(unit_f[:, 1, :], dst_nat, AX.X, ALU.max))
            v.tensor_reduce(group_f[:, 0:1], unit_f[:, 0, :], AX.X, ALU.min)
            link(v.tensor_reduce(group_f[:, 1:2], unit_f[:, 1, :], AX.X, ALU.max))
            link(v.tensor_scalar(unit_f, unit_f, -(WN - 1) / 2.0, 1.0 / WN, ALU.add, ALU.mult))
            v.tensor_copy(lies[0][0:NG, 0:2 * U * 2].bitcast(I32).rearrange("g (c u) -> g c u", c=2), unit_f).then_inc(s_dve, 1)
            chain[0] += 1
            dve.wait_ge(s_dve, chain[0])
            v.tensor_copy(unit_f, lies[0][0:NG, 0:2 * U * 2].bitcast(I32).rearrange("g (c u) -> g c u", c=2)).then_inc(s_unit_f, 1)
            half = (PT - 1) / 2.0
            link(v.tensor_scalar(group_f[:, 0:1], group_f[:, 0:1], -half, 1.0 / PT, ALU.add, ALU.mult))
            link(v.tensor_scalar(group_f[:, 1:2], group_f[:, 1:2], PT - half, 1.0 / PT, ALU.add, ALU.mult))
            v.tensor_scalar(group_b[:, 0:1], group_f[:, 0:1], 0.0, NB - 1.0, ALU.max, ALU.min)
            link(v.tensor_scalar(group_b[:, 1:2], group_f[:, 1:2], 1.0, float(NB), ALU.max, ALU.min))
            link(v.tensor_copy(group_f, group_b))
            v.scalar_tensor_tensor(group_i, group_f[:, 0:1], float(PACK), group_f[:, 1:2], ALU.mult, ALU.add).then_inc(s_group_i, 1)

            dve.wait_ge(s_edges, 48)
            link(v.tensor_scalar(hi_f, src_i, -half, 1.0 / PT, ALU.add, ALU.mult))
            link(v.tensor_copy(hi_i, hi_f))
            v.tensor_copy(dst_f[:], dst_i)
            link(v.tensor_copy(hi_f, hi_i))
            v.scalar_tensor_tensor(lo_f, hi_f, -float(PT), src_i, ALU.mult, ALU.add)
            v.scalar_tensor_tensor(key_f, dst_f[:], float(NB), hi_f, ALU.mult, ALU.add)
            v.scalar_tensor_tensor(typed_i, src_i, float(T), typ_i, ALU.mult, ALU.add).then_inc(s_typed, 1)

            dve.wait_ge(s_ids, 8)
            dve.wait_ge(s_scratch_in[0], 32)
            for h in range(2):
                w = window_id[:, h:h + 1]
                link(v.tensor_scalar(lies[h], unit_lo, w, None, ALU.is_le))
                link(v.scalar_tensor_tensor(met[h], unit_hi, w, lies[h], ALU.is_ge, ALU.mult))
                link(v.tensor_tensor(lies[h], met[h], unit_up, ALU.mult))
                v.tensor_reduce(window_f[:, h, 1:2], lies[h], AX.X, ALU.max)
                link(v.tensor_tensor(met[h], met[h], unit_down, ALU.mult))
                link(v.tensor_reduce(window_f[:, h, 0:1], met[h], AX.X, ALU.max))
            link(v.tensor_scalar(window_f[:, :, 0], window_f[:, :, 0], -1.0, float(NU), ALU.mult, ALU.add))
            link(v.tensor_scalar(window_f[:, :, 0], window_f[:, :, 0], float(NU - 1), None, ALU.min))
            link(v.scalar_tensor_tensor(window_f[:, :, 1], window_f[:, :, 0], 1.0, window_f[:, :, 1], ALU.add, ALU.max))
            link(v.tensor_scalar(window_f, window_f, float(U), None, ALU.mult))
            v.scalar_tensor_tensor(window_i, window_f[:, :, 0], float(PACK), window_f[:, :, 1], ALU.mult, ALU.add).then_inc(s_window_i, 1)

            units = dve.alloc_register("dve_units")
            place = dve.alloc_register("dve_place")
            span = [dve.alloc_register(f"dve_span{e}") for e in range(2)]
            dve.reg_mov(units, 0)
            dve.wait_ge(s_typed, 1)
            dve.wait_ge(s_scratch_in[2], 16)
            with dve.Fori(0, NW) as w:
                low, high = load_range(dve, window_bounds, w, NTILE, span)
                with dve.Fori(low, high, U) as k:
                    dve.reg_add(units, units, 1)
                    dve.wait_ge(s_unit_used, dve.snap(units, min_val=1))
                    dve.reg_alu(place, units, RING - 1, ALU.bitwise_and)
                    at_ring = dve.snap(place, min_val=0, max_val=RING - 1)
                    v.tensor_tensor(
                        lo_hot[:, bass.ds(at_ring * (U * H), U * H)].rearrange("p (u c) -> p u c", u=U)[:, :, 0:PT],
                        lo_ids[:, None, :].to_broadcast([PT, U, PT]),
                        lo_wide[:, bass.ds(k, U), None].to_broadcast([PT, U, PT]), ALU.is_equal)
                    v.scalar_tensor_tensor(
                        key_hot[:, bass.ds(at_ring * (U * KEYS), U * KEYS)].rearrange("p (u c) -> p u c", u=U),
                        key_ids[:, None, :].to_broadcast([PT, U, KEYS]), window_base[:, bass.ds(w, 1)],
                        key_wide[:, bass.ds(k, U), None].to_broadcast([PT, U, KEYS]),
                        ALU.add, ALU.is_equal).then_inc(s_unit, 1)

            dve.wait_ge(s_bank_free[0], NW // 2 + 2)
            dve.wait_ge(s_bank_free[1], NW // 2 + 1)
            v.tensor_reduce(over_col[:], over_parts, AX.X, ALU.add).then_inc(s_over_sum, 1)
            dve.wait_ge(s_over_sum, 2)
            v.tensor_scalar(over_flag[:], bank(7)[0:1, 0:1], 0.5, None, ALU.is_gt).then_inc(s_over, 1)
            dve.wait_ge(s_deg_turned, NC)
            link(v.tensor_scalar(rdeg[:], bank(0)[0:PT, 0:NB], 1.0, None, ALU.max))
            v.reciprocal(rdeg[:], rdeg[:]).then_inc(s_rdeg, 1)

            pairs = [dve.alloc_register(f"dve_pairs{h}") for h in range(2)]
            for h in range(2):
                dve.reg_mov(pairs[h], 0)
            dve.wait_ge(s_scratch_in[1], 16)

            def onehots(r):
                with dve.Fori(0, NG // 2) as i:
                    for h in range(2):
                        lo = h * G
                        low, high = load_range(dve, group_bounds, i * 2 + h, NB, span)
                        with dve.Fori(low, high) as b:
                            dve.reg_add(pairs[h], pairs[h], 1)
                            dve.wait_ge(s_onehot_used[h], dve.snap(pairs[h], min_val=1))
                            base = block_base[:, bass.ds(b, 1)]
                            mine = dst_f[:, bass.ds(i * (2 * G) + lo, G), None].to_broadcast([PT, G, PT])
                            ids = block_ids[:, None, :].to_broadcast([PT, G, PT])
                            last = v.scalar_tensor_tensor(onehot[:, lo:lo + G, :], ids, base, mine, ALU.add, ALU.is_equal)
                            if ROUNDS[r] == WEIGHTED:
                                link_dynamic(last, h)
                                scale = weight[:, bass.ds(i * (2 * G) + lo, G), None].to_broadcast([PT, G, PT])
                                last = v.tensor_tensor(onehot[:, lo:lo + G, :], onehot[:, lo:lo + G, :], scale, ALU.mult)
                            last.then_inc(s_onehot[h], 1)

            raw = dve.alloc_register("dve_raw_onehots")
            dve.reg_mov(raw, 0)

            def link_dynamic(ins, h):
                ins.then_inc(s_raw, 1)
                dve.reg_add(raw, raw, 1)
                dve.wait_ge(s_raw, dve.snap(raw, min_val=1))

            def sage_onehots(r, stage):
                over = dve.value_load(over_flag[0:1, 0:1], min_val=0, max_val=1)
                with dve.If(over > 0):
                    dve.wait_ge(s_p3, before(stage, SPLIT) + NC)
                    onehots(r)
                with dve.Else():
                    dve.nop()

            def evac(stage, r, i):
                j = ORDER[i]
                n, c = CHUNKS[j][1], evac_at(stage) + i
                dve.wait_ge(s_summed, r + 1)
                if i >= 2:
                    dve.wait_ge(s_lin, lin_at(stage) + i - 1)
                v.tensor_copy(agg[:, i % 2, 0:n * PT].rearrange("p (b c) -> p b c", c=PT), acc(j)).then_inc(s_evac, 1)

            def residue1(stage, i):
                c, n = spread_at(stage) + i, CHUNKS[ORDER[i]][1]
                b = CHUNKS[ORDER[i]][0]
                dve.wait_ge(s_h, c + 1)
                if before(stage, SPLIT) + i >= 2:
                    dve.wait_ge(s_p3, before(stage, SPLIT) + (i - 1 if i >= 2 else 0))
                v.tensor_tensor(tmp[0:PT, i % 2, 0:n * H], rows[0:PT, c % 2, 0:n * H],
                                parts[:, 0, b:b + n, :].rearrange("p b f -> p (b f)"), ALU.subtract).then_inc(s_r1, 1)

            def residue2(stage, i):
                b, n = CHUNKS[ORDER[i]]
                dve.wait_ge(s_p2, before(stage, SPLIT) + i + 1)
                v.tensor_tensor(parts[:, 2, b:b + n, :].rearrange("p b f -> p (b f)"), tmp[0:PT, i % 2, 0:n * H],
                                parts[:, 1, b:b + n, :].rearrange("p b f -> p (b f)"), ALU.subtract).then_inc(s_p3, 1)

            def combine(i, c, into):
                b, n = CHUNKS[ORDER[i]]
                for t in range(n):
                    o = slice(t * H, (t + 1) * H)
                    last = v.scalar_tensor_tensor(into[:, o], bank(ORDER[i])[0:PT, o], rdeg[:, b + t:b + t + 1],
                                                  into[:, o], ALU.mult, ALU.add)
                return last

            def sage_mid(r, stage):
                sage_onehots(r, SPREADS[SPREADS.index(stage) - 1])
                evac(stage, r, 0)
                for i in range(NC + 2):
                    if i + 1 < NC:
                        evac(stage, r, i + 1)
                    if i < NC:
                        c = spread_at(stage) + i
                        dve.wait_ge(s_root, ROOTS.index(stage) * NC + i + 1)
                        combine(i, c, rows[0:PT, c % 2]).then_inc(s_pre, 1)
                    if 1 <= i <= NC:
                        residue1(stage, i - 1)
                    if i >= 2:
                        residue2(stage, i - 2)

            def layer_norm(n):
                stage = f"N{n}"
                if n == 0:
                    dve.wait_ge(s_x, 16)
                else:
                    dve.wait_ge(s_resid, NC * n)
                for t in range(NB):
                    last = v.bn_stats(stats[:, t, :], x_rows[:, t, :])
                link(last)
                for t in range(NB):
                    last = v.bn_aggr(moments[:, t, :], stats[:, t, :])
                last.then_inc(s_std_in, 1)
                dve.wait_ge(s_std, n + 1)
                link(v.reciprocal(rstd[:], std[:]))
                split = stage in SPLIT
                for i in range(NC + 2 * split):
                    if i < NC:
                        b, m = CHUNKS[ORDER[i]]
                        c = spread_at(stage) + i
                        buffer_free(dve, c)
                        for t in range(m):
                            last = v.tensor_scalar(rows[0:PT, c % 2, t * H:(t + 1) * H], x_rows[:, b + t, :],
                                                   moments[:, b + t, 0:1], rstd[:, b + t:b + t + 1],
                                                   ALU.subtract, ALU.mult)
                        last.then_inc(s_pre, 1)
                    if split and 1 <= i <= NC:
                        residue1(stage, i - 1)
                    if split and i >= 2:
                        residue2(stage, i - 2)

            def final(n, r, stage):
                kind = ROUNDS[r]
                if kind != TYPED:
                    evac(stage, r, 0)
                for i in range(NC):
                    if kind != TYPED and i + 1 < NC:
                        evac(stage, r, i + 1)
                    b, m = CHUNKS[ORDER[i]]
                    c = NC * n + i
                    x_new = x_rows[:, b:b + m, :].rearrange("p b f -> p (b f)")
                    dve.wait_ge(s_lin, lin_at(stage) + i + 1)
                    x_wait = sum(x % 2 == c % 2 for x in range(c + 1))
                    dve.wait_ge(s_x_old[c % 2], 16 * x_wait)
                    if kind == SAGE:
                        dve.wait_ge(s_root, ROOTS.index(stage) * NC + i + 1)
                        link(combine(i, c, rows[0:PT, c % 2]))
                        v.tensor_tensor(x_new, rows[0:PT, c % 2, 0:m * H], tmp[0:PT, c % 2, 0:m * H], ALU.add).then_inc(s_resid, 1)
                    else:
                        src = root_bank(i) if kind == TYPED else bank(ORDER[i])
                        v.tensor_tensor(x_new, src[0:PT, 0:m * H], tmp[0:PT, c % 2, 0:m * H], ALU.add).then_inc(s_resid, 1)

            def typed_half(layer):
                for b in range(NB):
                    c = NB * layer + b
                    dve.wait_ge(s_tab, c + 1)
                    if c >= 2:
                        dve.wait_ge(s_staged[c % 2], 16 * (c // 2))
                    v.tensor_copy(table_stage[:, c % 2, BANK:2 * BANK], bank(2 * (b % 4) + 1)[0:PT, :]).then_inc(s_tab_v, 1)

            def gru(layer, r):
                dve.wait_ge(s_summed, r + 1)
                for j in range(0, NC, 2):
                    b, n = CHUNKS[j]
                    v.tensor_copy(aggT[:, b:b + n, :], acc(j)).then_inc(s_agg_v, 1)
                c0 = len(HALVES) * layer

                def first_part(c):
                    b, m = HALVES[c]
                    q, n = c % 2, m * PT
                    dve.wait_ge(s_act1, c0 + c + 1)
                    link(v.tensor_tensor(gate_r[:, q, 0:n], gate_r[:, q, 0:n], gate_n[:, q, 0:n], ALU.mult))
                    v.tensor_tensor(gate_r[:, q, 0:n], gate_r[:, q, 0:n], bank(2 * (c % 4) + 1)[:, 0:n],
                                    ALU.add).then_inc(s_dve1, 1)

                def second_part(c):
                    b, m = HALVES[c]
                    q, n = c % 2, m * PT
                    h = hT[:, b:b + m, 0:PT]
                    gz, gn = (g[:, q, 0:n].rearrange("p (b c) -> p b c", c=PT) for g in (gate_z, gate_n))
                    dve.wait_ge(s_act2, c0 + c + 1)
                    link(v.tensor_tensor(h, h, gn, ALU.subtract))
                    link(v.tensor_tensor(h, h, gz, ALU.mult))
                    link(v.tensor_tensor(h, h, gn, ALU.add))
                    v.tensor_scalar(h, h, 0.0, None, ALU.max).then_inc(s_gru, 1)

                for c in range(len(HALVES) + 1):
                    if c < len(HALVES):
                        first_part(c)
                    if c:
                        second_part(c - 1)

            dve.wait_ge(s_small, 16 * 2)
            v.tensor_tensor(b_rz[:], b_gru[:, :, 0, 0:2], b_gru[:, :, 1, 0:2], ALU.add).then_inc(s_const, 1)
            layer_norm(0)
            sage_mid(0, "M0")
            sage_mid(1, "M1")
            sage_onehots(2, "M1")
            final(0, 2, "F0")
            layer_norm(1)
            for layer in range(2):
                typed_half(layer)
                onehots(3 + layer)
                gru(layer, 3 + layer)
            final(1, 4, "F1")
            layer_norm(2)
            sage_mid(5, "M5")
            sage_mid(6, "M6")
            sage_onehots(7, "M6")
            final(2, 7, "F2")
            layer_norm(3)
            dve.wait_ge(s_index[8], 32)
            onehots(8)
            final(3, 8, "F3")

        @block.tensor
        def _(pe):
            mm = nc.tensor.matmul
            pe.wait_ge(s_const, 1)
            pe.sem_inc(s_unit_used, RING)
            for h in range(2):
                pe.sem_inc(s_onehot_used[h], 1)
                pe.sem_inc(s_free[h], 1)

            units = pe.alloc_register("pe_units")
            span = [pe.alloc_register(f"pe_span{e}") for e in range(2)]
            place = pe.alloc_register("pe_place")
            taken = pe.alloc_register("pe_windows")
            pe.reg_mov(units, 0)
            pe.wait_ge(s_scratch_in[2], 16)

            def window(w, q, wait):
                low, high = load_range(pe, window_bounds, w, NTILE, span)
                o = bank(q)[0:PT, 0:KEYS]
                pe.wait_ge(s_bank_free[q], wait)
                mm(o, zeros[:, 0:PT], zero_keys, start=True, stop=False)
                with pe.Fori(low, high, U) as k:
                    pe.reg_add(units, units, 1)
                    pe.wait_ge(s_unit, pe.snap(units, min_val=1))
                    pe.reg_alu(place, units, RING - 1, ALU.bitwise_and)
                    at_ring = pe.snap(place, min_val=0, max_val=RING - 1)
                    for u in range(U):
                        last = mm(o, lo_hot[:, bass.ds(at_ring * (U * H) + u * H, PT)],
                                  key_hot[:, bass.ds(at_ring * (U * KEYS) + u * KEYS, KEYS)], start=False, stop=False)
                    last.then_inc(s_unit_used, 1)
                mm(o, zeros[:, 0:PT], zero_keys, start=False, stop=True).then_inc(s_window, 1)

            pe.sem_inc(s_bank_free[0], 1)
            pe.sem_inc(s_bank_free[1], 1)
            with pe.Fori(0, NW // 2) as i:
                for q in range(2):
                    window(i * 2 + q, q, i + 1)
            window(NW - 1, 0, NW // 2 + 1)

            def turn_degrees(j):
                b, n = CHUNKS[j]
                pe.wait_ge(s_deg_row, j + 1)
                for t in range(n):
                    last = mm(bank(0)[0:PT, b + t:b + t + 1], deg_row[:, j % 2, t * PT:(t + 1) * PT], ones[0:1, 0:1],
                              start=True, stop=True)
                last.then_inc(s_deg_turned, 1)

            pe.wait_ge(s_over_sum, 1)
            mm(bank(7)[0:1, 0:1], over_col[:], ones[:, 0:1], start=True, stop=True).then_inc(s_over_sum, 1)
            pe.wait_ge(s_counted, NW)
            for j, (b, n) in enumerate(CHUNKS):
                o = bank(1 + j % 2)[0:1, 0:n * PT]
                if j >= 2:
                    pe.wait_ge(s_deg_row, j - 1)
                for t in range(NB):
                    last = mm(o, ones_bf[:, 0:1], counts[:, t, b * PT:(b + n) * PT], start=t == 0, stop=t == NB - 1)
                last.then_inc(s_deg, 1)
                if j:
                    turn_degrees(j - 1)
            turn_degrees(NC - 1)

            pairs = [pe.alloc_register(f"pe_pairs{h}") for h in range(2)]
            groups = [pe.alloc_register(f"pe_groups{h}") for h in range(2)]
            for h in range(2):
                pe.reg_mov(pairs[h], 0)
                pe.reg_mov(groups[h], 1)
            pe.wait_ge(s_scratch_in[1], 16)

            def open_sums():
                for j in range(NC):
                    mm(bank(j).rearrange("p (b c) -> p b c", c=H), zeros[:], zeros[:, None, :].to_broadcast([1, 4, H]),
                       start=True, stop=False)

            def close_sums():
                for j in range(NC):
                    last = mm(bank(j).rearrange("p (b c) -> p b c", c=H), zeros[:], zeros[:, None, :].to_broadcast([1, 4, H]),
                              start=False, stop=True)
                last.then_inc(s_summed, 1)

            def sum_gathered():
                with pe.Fori(0, NG // 2) as i:
                    for h in range(2):
                        lo = h * G
                        low, high = load_range(pe, group_bounds, i * 2 + h, NB, span)
                        pe.wait_ge(s_gathered[h], pe.snap(groups[h], min_val=1) * (16 * G))
                        pe.reg_add(groups[h], groups[h], 1)
                        with pe.Fori(low, high) as b:
                            pe.reg_add(pairs[h], pairs[h], 1)
                            pe.wait_ge(s_onehot[h], pe.snap(pairs[h], min_val=1))
                            for s in range(lo, lo + G):
                                last = mm(psum[:, bass.ds(b * H, PT)], msg[:, s, :], onehot[:, s, :], start=False, stop=False)
                            last.then_inc(s_onehot_used[h], 1)
                        mm(spare, zeros[:, 0:1], zeros[:, 0:1], start=True, stop=True).then_inc(s_free[h], 1)

            def sum_dense(stage):
                for i, j in enumerate(ORDER):
                    b, n = CHUNKS[j]
                    pe.wait_ge(s_p3, before(stage, SPLIT) + i + 1)
                    with pe.Fori(b, b + n) as t:
                        for k in range(3):
                            part = parts[:, k, bass.ds(t, 1), :].rearrange("p b f -> p (b f)")
                            for jj, (bb, m) in enumerate(CHUNKS):
                                mm(acc(jj), part,
                                   counts[:, bass.ds(t, 1), bb * PT:(bb + m) * PT].rearrange("p a (b c) -> p (a b) c", c=PT),
                                   start=False, stop=False)

            def sage(r, stage):
                over = pe.value_load(over_flag[0:1, 0:1], min_val=0, max_val=1)
                pe.wait_ge(s_turned, before(stage, TURNED) + NC)
                open_sums()
                with pe.If(over > 0):
                    sum_gathered()
                with pe.Else():
                    sum_dense(stage)
                close_sums()

            def transpose_rows(stage, i):
                c, n = spread_at(stage) + i, CHUNKS[ORDER[i]][1]
                pe.wait_ge(s_h, c + 1)
                for t in range(n):
                    last = nc.tensor.transpose(turned_bank(i)[:, t * PT:(t + 1) * PT], rows[0:PT, c % 2, t * H:(t + 1) * H],
                                               ident[0:PT, 0:PT])
                last.then_inc(s_trans, 1)

            def linear(stage, i, w, bias, banks_free):
                j = ORDER[i]
                b, n = CHUNKS[j]
                if w[1] is not None:
                    banks_free(i)
                    for t in range(n):
                        o = root_bank(i)[0:PT, t * H:(t + 1) * H]
                        mm(o, hT[:, b + t, 0:PT], w[1], start=True, stop=False)
                        last = mm(o, ones[32 * bias:32 * bias + 1, 0:PT], b_rows[32 * bias:32 * bias + 1, :], start=False, stop=True)
                if w[0] is not None:
                    pe.wait_ge(s_evac, evac_at(stage) + i + 1)
                    for t in range(n):
                        last = mm(bank(j)[0:PT, t * H:(t + 1) * H], agg[:, i % 2, t * PT:(t + 1) * PT], w[0],
                                  start=True, stop=True)
                last.then_inc(s_lin, 1)

            def w_of(n):
                return w_layer[:, n * H:(n + 1) * H]

            def sage_mid(r, stage, n):
                def banks_free(i):
                    if i >= 2:
                        pe.wait_ge(s_root, ROOTS.index(stage) * NC + i - 1)
                    if i == 2:
                        pe.wait_ge(s_turned, before(stage, TURNED) + 1)
                    if i == 1:
                        pe.wait_ge(s_pre, spread_at(stage) + 1)

                for i in range(NC + 1):
                    if i < NC:
                        linear(stage, i, (w_of(2 * n), w_of(2 * n + 1)), n, banks_free)
                    if i:
                        transpose_rows(stage, i - 1)

            def final(n, stage, w, bias):
                def banks_free(i):
                    if i >= 1:
                        pe.wait_ge(s_resid, NC * n + (i - 1 if i >= 2 else 1))

                for i in range(NC):
                    linear(stage, i, w, bias, banks_free)

            def turn_norm(stage):
                for i in range(NC):
                    transpose_rows(stage, i)

            def typed_products(layer):
                pe.wait_ge(s_types_w[layer], 16)
                for b in range(NB):
                    c = NB * layer + b
                    if b >= 4:
                        pe.wait_ge(s_tab_a, c - 3)
                        pe.wait_ge(s_tab_v, c - 3)
                    for q in range(2):
                        last = mm(bank(2 * (b % 4) + q)[0:PT, :], hT[:, b, 0:PT], w_types[:, q * BANK:(q + 1) * BANK],
                                  start=True, stop=True)
                    last.then_inc(s_tab, 1)

            def gru(layer):
                pe.wait_ge(s_agg_v, (NC + 1) // 2 * (layer + 1))
                pe.wait_ge(s_agg_a, NC // 2 * (layer + 1))
                pe.wait_ge(s_layer_w[1 + layer], 32 if layer == 0 else 16)
                c0 = len(HALVES) * layer
                for c, (b, m) in enumerate(HALVES):
                    n = m * PT
                    if c >= 4:
                        pe.wait_ge(s_dve1, c0 + c - 3)
                    x, h = aggT[:, b:b + m, :], hT[:, b:b + m, 0:PT]
                    rz, nn = bank(2 * (c % 4)), bank(2 * (c % 4) + 1)
                    for g in range(2):
                        o = rz[:, g * 2 * PT:g * 2 * PT + n]
                        mm(o, w_layer[:, g * H:(g + 1) * H], x, start=True, stop=False)
                        mm(o, w_layer[:, (3 + g) * H:(4 + g) * H], h, start=False, stop=True)
                    mm(nn[:, 0:n], w_of(2), x, start=True, stop=True)
                    mm(nn[:, 2 * PT:2 * PT + n], w_of(5), h, start=True, stop=True).then_inc(s_gates, 1)

            pe.wait_ge(s_ident, 1)
            pe.wait_ge(s_layer_w[0], 64)
            pe.wait_ge(s_rdeg, 1)
            turn_norm("N0")
            sage(0, "N0")
            sage_mid(0, "M0", 0)
            sage(1, "M0")
            sage_mid(1, "M1", 1)
            sage(2, "M1")
            final(0, "F0", (w_of(4), w_of(5)), 2)
            turn_norm("N1")
            pe.wait_ge(s_turned, before("N1", TURNED) + NC)
            pe.wait_ge(s_single_w[0], 16)
            for i, (b, m) in enumerate(CHUNKS):
                mm(bank(i)[:, 0:m * PT], w_single[:], hT[:, b:b + m, 0:PT], start=True, stop=True).then_inc(s_proj, 1)
            pe.wait_ge(s_projed, NC)
            for layer in range(2):
                typed_products(layer)
                pe.wait_ge(s_tab_a, NB * (layer + 1))
                pe.wait_ge(s_tab_v, NB * (layer + 1))
                open_sums()
                sum_gathered()
                close_sums()
                gru(layer)
                pe.wait_ge(s_gru, len(HALVES) * (layer + 1))
            pe.wait_ge(s_single_w[1], 16)
            final(1, "F1", (None, w_single[:]), 0)
            turn_norm("N2")
            pe.wait_ge(s_layer_w[3], 64)
            sage(5, "N2")
            sage_mid(5, "M5", 0)
            sage(6, "M5")
            sage_mid(6, "M6", 1)
            sage(7, "M6")
            final(2, "F2", (w_of(4), w_of(5)), 2)
            pe.wait_ge(s_resid, NC * 3)
            pe.wait_ge(s_single_w[2], 16)
            open_sums()
            sum_gathered()
            close_sums()
            final(3, "F3", (w_single[:], None), None)

        @block.scalar
        def _(act):
            act.dma_start(w_layer[:], a["w_sage0"]).then_inc(s_layer_w[0], 16)
            for n in range(3):
                act.dma_start(b_rows[32 * n:32 * n + 1, :], a["b_sage0"][n:n + 1, :]).then_inc(s_layer_w[0], 16)
            act.dma_start(b_proj[:], a["b_proj"]).then_inc(s_small, 16)
            act.dma_start(b_gru[:], a["b_gru"]).then_inc(s_small, 16)
            act.dma_start(w_single[:], a["w_proj"]).then_inc(s_single_w[0], 16)
            fn = nc.scalar.activation

            act.wait_ge(s_const, 1)

            def take_window(w, q, n):
                o = bank(q)[0:PT, 0:n * NB]
                fn(counts[:, :, bass.ds(w * WN, n)].rearrange("p h d -> p d h"),
                   o.rearrange("p (d h) -> p d h", h=NB), ACT.Copy).then_inc(s_counted, 1)
                fn(o, o, ACT.Relu, bias=over_col[:], accum_out=over_parts[:, bass.ds(w, 1)]).then_inc(s_bank_free[q], 1)

            with act.Fori(0, NW // 2) as i:
                for q in range(2):
                    act.wait_ge(s_window, i * 2 + q + 1)
                    take_window(i * 2 + q, q, WN)
            act.wait_ge(s_window, NW)
            take_window(NW - 1, 0, N - (NW - 1) * WN)

            for j, (b, n) in enumerate(CHUNKS):
                act.wait_ge(s_deg, j + 1)
                if j >= 2:
                    act.wait_ge(s_deg_turned, j - 1)
                fn(deg_row[:, j % 2, 0:n * PT], bank(1 + j % 2)[0:1, 0:n * PT], ACT.Copy).then_inc(s_deg_row, 1)

            def root(n):
                act.wait_ge(s_std_in, n + 1)
                fn(std[:], moments[:, :, 1], ACT.Sqrt, bias=eps_col[:]).then_inc(s_std, 1)

            def take_root(stage, i, c):
                act.wait_ge(s_lin, lin_at(stage) + i + 1)
                n = CHUNKS[ORDER[i]][1] * H
                fn(rows[0:PT, c % 2, 0:n], root_bank(i)[0:PT, 0:n], ACT.Copy).then_inc(s_root, 1)

            def final_roots(n, stage):
                free_at = spread_at(f"N{n + 1}")
                buffer_free(act, free_at)
                buffer_free(act, free_at + 1)
                for i in range(NC):
                    c = NC * n + i
                    if i >= 2:
                        act.wait_ge(s_resid, c - 1)
                    take_root(stage, i, c)

            def spread(stage):
                split, turned = stage in SPLIT, stage in TURNED
                inner = stage[0] == "M"
                if inner:
                    buffer_free(act, spread_at(stage))
                    take_root(stage, 0, spread_at(stage))
                    buffer_free(act, spread_at(stage) + 1)
                    take_root(stage, 1, spread_at(stage) + 1)
                for i in range(NC + 1):
                    if i < NC:
                        b, n = CHUNKS[ORDER[i]]
                        c = spread_at(stage) + i
                        act.wait_ge(s_pre, c + 1)
                        mine = rows[0:PT, c % 2, 0:n * H]
                        if split:
                            fn(parts[:, 0, b:b + n, :].rearrange("p b f -> p (b f)"), mine, ACT.Relu)
                        fn(mine, mine, ACT.Relu).then_inc(s_h, 1)
                    if i:
                        b, n = CHUNKS[ORDER[i - 1]]
                        if turned:
                            if i == 1 and stage[0] == "N" and stage != "N0":
                                act.wait_ge(s_x_out[int(stage[1]) - 1], 16 * NC)
                            if i == 1 and stage[0] == "N":
                                act.wait_ge(s_pre, spread_at(stage) + 1)
                            act.wait_ge(s_trans, before(stage, TURNED) + i)
                            fn(hT[:, b:b + n, 0:PT], turned_bank(i - 1)[:, 0:n * PT].rearrange("p (b c) -> p b c", c=PT),
                               ACT.Copy).then_inc(s_turned, 1)
                        if split:
                            act.wait_ge(s_r1, before(stage, SPLIT) + i)
                            fn(parts[:, 1, b:b + n, :].rearrange("p b f -> p (b f)"), tmp[0:PT, (i - 1) % 2, 0:n * H],
                               ACT.Copy).then_inc(s_p2, 1)
                        if inner and i + 1 < NC:
                            buffer_free(act, spread_at(stage) + i + 1)
                            take_root(stage, i + 1, spread_at(stage) + i + 1)

            def typed_half(layer):
                for b in range(NB):
                    c = NB * layer + b
                    act.wait_ge(s_tab, c + 1)
                    if c >= 2:
                        act.wait_ge(s_staged[c % 2], 16 * (c // 2))
                    fn(table_stage[:, c % 2, 0:BANK], bank(2 * (b % 4))[0:PT, :], ACT.Copy).then_inc(s_tab_a, 1)

            def gru(layer, r):
                act.wait_ge(s_summed, r + 1)
                for j in range(1, NC, 2):
                    b, n = CHUNKS[j]
                    fn(aggT[:, b:b + n, :], acc(j), ACT.Copy).then_inc(s_agg_a, 1)
                c0 = len(HALVES) * layer

                def gate(c):
                    n = HALVES[c][1] * PT
                    q = c % 2
                    rz, nn = bank(2 * (c % 4)), bank(2 * (c % 4) + 1)
                    act.wait_ge(s_gates, c0 + c + 1)
                    if c >= 2:
                        act.wait_ge(s_gru, c0 + c - 1)
                    fn(gate_r[:, q, 0:n], rz[:, 0:n], ACT.Sigmoid, bias=b_rz[:, layer, 0:1])
                    fn(gate_z[:, q, 0:n], rz[:, 2 * PT:2 * PT + n], ACT.Sigmoid, bias=b_rz[:, layer, 1:2])
                    fn(gate_n[:, q, 0:n], nn[:, 2 * PT:2 * PT + n], ACT.Identity,
                       bias=b_gru[:, layer, 1, 2:3]).then_inc(s_act1, 1)

                def candidate(c):
                    n = HALVES[c][1] * PT
                    act.wait_ge(s_dve1, c0 + c + 1)
                    fn(gate_n[:, c % 2, 0:n], gate_r[:, c % 2, 0:n], ACT.Tanh,
                       bias=b_gru[:, layer, 0, 2:3]).then_inc(s_act2, 1)

                for c in range(len(HALVES) + 1):
                    if c < len(HALVES):
                        gate(c)
                    if c:
                        candidate(c - 1)

            root(0)
            spread("N0")
            spread("M0")
            spread("M1")
            final_roots(0, "F0")
            root(1)
            spread("N1")
            for j, (b, m) in enumerate(CHUNKS):
                act.wait_ge(s_proj, j + 1)
                fn(hT[:, b:b + m, 0:PT], bank(j)[:, 0:m * PT].rearrange("p (b c) -> p b c", c=PT), ACT.Relu,
                   bias=b_proj[:]).then_inc(s_projed, 1)
            act.wait_ge(s_const, 2)
            for layer in range(2):
                typed_half(layer)
                gru(layer, 3 + layer)
            root(2)
            spread("N2")
            spread("M5")
            spread("M6")
            final_roots(2, "F2")
            root(3)
            spread("N3")


def laid_out(i):
    import numpy as np

    def tiles(v):
        return v.reshape(NTILE, PT).T

    i = {k: np.asarray(v) for k, v in i.items()}
    sage0 = [i[f"L0_gnn_W{k}{n}"].T for n in range(3) for k in "lr"]
    sage2 = [i[f"L2_gnn_W{k}"][n] for n in range(3) for k in "lr"]
    put = {
        "dst_rows": i["dst"].reshape(NG, G * PT), "dst_t": tiles(i["dst"]), "src_t": tiles(i["src"]),
        "typ_t": tiles(i["edge_type_8"]), "weight_t": tiles(i["edge_weight"]), "x": i["x"],
        "w_sage0": np.concatenate(sage0, 1), "w_sage2": np.concatenate(sage2, 1),
        "b_sage0": np.stack([i[f"L0_gnn_bl{n}"] for n in range(3)]), "b_sage2": i["L2_gnn_b"],
        "b_out": i["L1_gnn_out_b"][None], "b_proj": i["L1_gnn_node_proj_b"][:, None],
        "b_gru": np.stack([i["L1_gnn_gru_bih"], i["L1_gnn_gru_bhh"]]).reshape(2, 2, 3, H).transpose(3, 1, 0, 2),
        "w_proj": i["L1_gnn_node_proj_w"].T, "w_out": i["L1_gnn_out_w"].T, "w_last": i["L3_gnn_W"].T,
    }
    for n in range(2):
        put[f"w_gru{n}"] = np.concatenate([i["L1_gnn_gru_wih"][n].T, i["L1_gnn_gru_whh"][n].T], 1)
        put[f"w_types{n}"] = i["L1_gnn_edge_W"][n].transpose(2, 0, 1).reshape(H, T * H)
    return {k: np.ascontiguousarray(v) for k, v in put.items()}


def kernel(**inputs):
    import concourse.bacc as bacc
    from concourse.bass_utils import run_bass_kernel_spmd

    arrays = laid_out(inputs)
    nc = bacc.Bacc("TRN2", target_bir_lowering=False, num_devices=1)
    aps = {k: nc.dram_tensor(f"in_{k}", v.shape, mybir.dt.from_np(v.dtype), kind="ExternalInput").ap()
           for k, v in arrays.items()}
    out = nc.dram_tensor("out_x", (N, H), F32, kind="ExternalOutput").ap()
    gnn_program(nc, aps, out)
    got = run_bass_kernel_spmd(nc, [{f"in_{k}": v for k, v in arrays.items()}], core_ids=[0])
    return got.results[0]["out_x"]
```

```python
from contextlib import ExitStack

import concourse.bass as bass
from concourse import mybir

F32 = mybir.dt.float32
F16 = mybir.dt.float16
BF16 = mybir.dt.bfloat16
I32 = mybir.dt.int32
U32 = mybir.dt.uint32
ALU = mybir.AluOpType
ACT = mybir.ActivationFunctionType
AX = mybir.AxisListType

N, E, H, T = 3125, 100000, 128, 8
PT = 125
NB = N // PT
NTILE = E // PT
G = 8
NG = NTILE // G
SLOTS = 4
U = 2
NU = NTILE // U
WN = 20
NW = (N + WN - 1) // WN
WL = 4
TAIL = NW // WL * WL
KEYS = WN * NB
RING = 4
PACK = 1024
PACK_BITS = PACK.bit_length() - 1
EPS = 1e-5
BANK = 512
CHUNKS = [(4 * j, min(4, NB - 4 * j)) for j in range((NB + 3) // 4)]
NC = len(CHUNKS)
ORDER = [NC - 1] + list(range(NC - 1))
HALVES = [(NB - 1, 1)] + [(2 * c, 2) for c in range(NB // 2)]
GRU_STEPS = 3
GRU_PAIRS = 3

SAGE, TYPED, WEIGHTED = "sage", "typed", "weighted"
ROUNDS = [SAGE, SAGE, SAGE, TYPED, TYPED, SAGE, SAGE, SAGE, WEIGHTED]
FINAL_ROUND = [2, 4, 7, 8]
SPREADS = ["N0", "M0", "M1", "N1", "N2", "M5", "M6", "N3"]
STORED = ["N0", "M0", "M1", "N2", "M5", "M6", "N3"]
SPLIT = ["N0", "M0", "M1", "N2", "M5", "M6"]
TURNED = [x for x in SPREADS if x != "N3"]


def gnn_program(nc, a, out):
    ctx = ExitStack()
    with ctx:
        def sb(name, shape, dt=F32):
            return ctx.enter_context(nc.sbuf_tensor(name, shape, dt))

        def sem(name):
            return ctx.enter_context(nc.semaphore(name))

        def two(name):
            return [sem(f"{name}{q}") for q in range(2)]

        def dram(name, shape, dt=F32):
            return nc.dram_tensor(name, shape, dt).ap()

        node_table = dram("node_table", (N, H))
        typed_table = dram("typed_table", (N * T, H))
        x_dram = dram("x_dram", (N, H))
        typed_index = dram("typed_index", (PT, NTILE), I32)
        group_scratch = dram("group_scratch", (NG, 1), I32)
        unit_scratch = dram("unit_scratch", (2, NU))
        window_scratch = dram("window_scratch", (2 * H, 1), I32)

        counts = sb("counts", [PT, NB, N], BF16)
        dst_f = sb("dst_f", [PT, NTILE])
        group_bounds = sb("group_bounds", [1, NG], I32)
        w_layer = sb("w_layer", [H, 6 * H])
        w_single = sb("w_single", [H, H])
        b_rows = sb("b_rows", [3 * 32, H])
        b_proj = sb("b_proj", [H, 1])
        b_gru = sb("b_gru", [H, 2, 2, 3])
        b_rz = sb("b_rz", [H, 2, 2])
        ident = sb("ident", [H, H])
        ones = sb("ones", [PT, H])
        zeros = sb("zeros", [1, H], BF16)
        block_ids = sb("block_ids", [PT, PT])
        block_base = sb("block_base", [PT, NB])
        rdeg = sb("rdeg", [PT, NB])
        moments = sb("moments", [PT, NB, 2])
        std = sb("std", [PT, NB])
        rstd = sb("rstd", [PT, NB])
        eps_col = sb("eps_col", [PT, 1])
        over_col = sb("over_col", [PT, 1])
        over_flag = sb("over_flag", [1, 1], I32)
        WORK_R, WORK_ROWS, WORK_AGG, WORK_TMP, WORK_U = NB * H, 2 * BANK, 2 * BANK, 2 * BANK, 5120
        work = sb("work", [H, WORK_R + WORK_ROWS + WORK_AGG + WORK_TMP + WORK_U])
        at = [0]

        def carve(size):
            at[0] += size
            return work[:, at[0] - size:at[0]]

        def blocks(v, dt=F32):
            return v.rearrange("p (b c) -> p b c", c=H)

        region = blocks(carve(WORK_R))
        rows = carve(WORK_ROWS).rearrange("p (q c) -> p q c", q=2)
        agg = carve(WORK_AGG).rearrange("p (q c) -> p q c", q=2)
        tmp = carve(WORK_TMP).rearrange("p (q c) -> p q c", q=2)
        union = carve(WORK_U)
        x_rows = region[0:PT]
        hT = region
        w_types = work[:, WORK_R + WORK_ROWS:WORK_R + WORK_ROWS + T * H]
        stats = union[0:PT, WORK_U - NB * 6:WORK_U].rearrange("p (b s) -> p b s", s=6)
        parts = union[0:PT, 0:3 * NB * H // 2].bitcast(BF16).rearrange("p (k b f) -> p k b f", k=3, f=H)
        msg = [v.rearrange("p (s f) -> p s f", f=H) for v in (
            union[0:PT, 0:G * H], union[0:PT, G * H:2 * G * H],
            rows[0:PT].rearrange("p q c -> p (q c)"), tmp[0:PT].rearrange("p q c -> p (q c)"))]
        assert len(msg) == SLOTS and NG % SLOTS == 0 and 2 * BANK == G * H
        onehot = union[0:PT, 2048:2048 + 2 * G * PT].rearrange("p (s c) -> p s c", c=PT)
        index = union[0:PT, 4096:4096 + NTILE].bitcast(I32)
        ring = union[0:PT, 4096 + NTILE:4096 + NTILE + SLOTS * G].bitcast(U32)
        weight = region[0:PT].rearrange("p b c -> p (b c)")[:, 0:NTILE]
        table_stage = union[0:PT, 0:2 * T * H].rearrange("p (q c) -> p q c", q=2)
        aggT = union[:, 0:N].rearrange("p (b c) -> p b c", c=PT)
        STEP = 2 * PT
        gates = [union[:, 3200:3200 + 3 * STEP], union[:, 3200 + 3 * STEP:3200 + 6 * STEP],
                 rows.rearrange("p q c -> p (q c)")[:, 0:3 * STEP]]
        gate_r, gate_z, gate_n = ([v[:, k * STEP:(k + 1) * STEP] for v in gates] for k in range(3))
        at[0] = 0
        dst_i = carve(NTILE)[0:PT].bitcast(I32)
        src_i = carve(NTILE)[0:PT].bitcast(I32)
        typ_i = carve(NTILE)[0:PT].bitcast(I32)
        dst_nat = carve(G * PT)[0:NG].bitcast(I32).rearrange("g (u e) -> g u e", e=U * PT)
        hi_f = carve(NTILE)[0:PT]
        lo_wide = carve((NTILE + U) // 2)[0:PT].bitcast(F16)
        key_wide = carve(NTILE + U)[0:PT]
        lo_f, key_f = lo_wide[:, 0:NTILE], key_wide[:, 0:NTILE]
        typed_i = carve(NTILE)[0:PT].bitcast(I32)
        unit_lo = carve(NU)
        unit_hi = carve(NU)
        unit_up = carve(NU)
        unit_down = carve(NU)
        deg_row = work[0:1, at[0] - 4 * NU:at[0] - 4 * NU + 2 * BANK].rearrange("p (q c) -> p q c", q=2)
        lies = [carve(NU) for _ in range(2)]
        met = [carve(NU) for _ in range(2)]
        hi_i = work[0:PT, at[0] - 2 * NU:at[0]].bitcast(I32)
        window_id = carve(2)
        window_f = carve(4).rearrange("p (h c) -> p h c", c=2)
        window_i = carve(2).bitcast(I32)
        unit_f = carve(2 * U * 2)[0:NG].rearrange("g (c u) -> g c u", c=2)
        unit_i = carve(2 * U * 2)[0:NG].bitcast(I32).rearrange("g (c u) -> g c u", c=2)
        group_f = carve(2)[0:NG]
        group_b = carve(2)[0:NG].bitcast(I32)
        group_i = carve(1)[0:NG].bitcast(I32)
        window_base = carve(NW)[0:PT]
        window_bounds = carve(2 * H)[0:1].bitcast(I32)
        key_ids = carve(KEYS // 2)[0:PT].bitcast(F16)
        lo_ids = carve(64)[0:PT].bitcast(F16)[:, 0:PT]
        key_size, lo_size = RING * U * KEYS // 2, RING * U * H // 2
        assert NU * 2 == NTILE and key_size + lo_size <= 3 * NTILE + G * PT
        key_hot = work[0:PT, 0:key_size].bitcast(BF16)
        lo_hot = work[0:PT, key_size:key_size + lo_size].bitcast(BF16)
        zero_keys = carve(KEYS // 2)[0:1].bitcast(BF16)
        over_parts = carve(NW)[0:PT]
        ones_bf = carve(H // 2)[0:PT].bitcast(BF16)
        assert at[0] <= WORK_R + 3 * 2 * BANK + WORK_U - NB * 6, at[0]

        psum = ctx.enter_context(nc.psum_tensor("psum", [H, 8 * BANK], F32))

        def bank(j):
            return psum[:, j * BANK:(j + 1) * BANK]

        def acc(j):
            n = CHUNKS[j][1]
            return bank(j)[:, 0:n * H].rearrange("p (b c) -> p b c", c=H)[:, :, 0:PT]

        def root_bank(i):
            return bank(7 if i % 2 == 0 else NC - 1)

        def table_bank(b, q):
            return bank(2 * ((b + 3) % 4) + q)

        def turned_bank(i):
            return bank(7 if i == 0 else ORDER[i])

        spare = bank(7)[0:1, BANK - 1:BANK]

        s_dst, s_edges, s_x = sem("s_dst"), sem("s_edges"), sem("s_x")
        s_small = sem("s_small")
        s_layer_w = [sem(f"s_layer_w{n}") for n in range(4)]
        s_single_w = [sem(f"s_single_w{n}") for n in range(3)]
        s_types_w = two("s_types_w")
        s_const, s_ids, s_ident = sem("s_const"), sem("s_ids"), sem("s_ident")
        s_dve, s_pool = sem("s_dve"), sem("s_pool")
        s_unit_f, s_group_i, s_window_i, s_typed = sem("s_unit_f"), sem("s_group_i"), sem("s_window_i"), sem("s_typed")
        s_scratch_out = [sem(f"s_scratch_out{n}") for n in range(3)]
        s_scratch_in = [sem(f"s_scratch_in{n}") for n in range(3)]
        s_typed_out = sem("s_typed_out")
        s_unit, s_unit_used = sem("s_unit"), sem("s_unit_used")
        s_window, s_counted, s_bank_free = sem("s_window"), sem("s_counted"), two("s_bank_free")
        s_raw = sem("s_raw")
        s_over_sum, s_over = sem("s_over_sum"), sem("s_over")
        s_deg, s_deg_row, s_deg_turned, s_rdeg = sem("s_deg"), sem("s_deg_row"), sem("s_deg_turned"), sem("s_rdeg")
        s_index = [sem(f"s_index{r}") for r in range(len(ROUNDS))]
        s_ring = sem("s_ring")
        s_onehot, s_onehot_used = two("s_onehot"), two("s_onehot_used")
        s_free = [sem(f"s_free{q}") for q in range(SLOTS)]
        s_gathered = [sem(f"s_gathered{q}") for q in range(SLOTS)]
        s_summed = sem("s_summed")
        s_evac = sem("s_evac")
        s_lin = sem("s_lin")
        s_pre, s_h, s_r1, s_p2, s_p3 = sem("s_pre"), sem("s_h"), sem("s_r1"), sem("s_p2"), sem("s_p3")
        s_root = sem("s_root")
        s_trans, s_turned = sem("s_trans"), sem("s_turned")
        s_stored = two("s_stored")
        s_std_in, s_std = sem("s_std_in"), sem("s_std")
        s_resid = sem("s_resid")
        s_x_old = two("s_x_old")
        s_x_out = [sem(f"s_x_out{n}") for n in range(4)]
        s_proj, s_projed = sem("s_proj"), sem("s_projed")
        s_tab, s_tab_a, s_tab_v = sem("s_tab"), sem("s_tab_a"), sem("s_tab_v")
        s_staged = two("s_staged")
        s_agg_a, s_agg_v = sem("s_agg_a"), sem("s_agg_v")
        s_gates, s_act1, s_dve1, s_act2, s_gru = sem("s_gates"), sem("s_act1"), sem("s_dve1"), sem("s_act2"), sem("s_gru")

        block = ctx.enter_context(nc.Block())

        def spread_at(stage):
            return NC * SPREADS.index(stage)

        def before(stage, kinds):
            return NC * sum(x in kinds for x in SPREADS[:SPREADS.index(stage)])

        def stores_before(stage, q):
            n = 0
            for x in SPREADS[:SPREADS.index(stage)]:
                n += sum(x in STORED and (spread_at(x) + i) % 2 == q for i in range(NC))
            return n

        LIN_ROUNDS = ["M0", "M1", "F0", "F1", "M5", "M6", "F2", "F3"]
        EVAC_ROUNDS = [x for x in LIN_ROUNDS if x != "F1"]

        ROOTS = ["M0", "M1", "F0", "M5", "M6", "F2"]

        def lin_at(stage):
            return NC * LIN_ROUNDS.index(stage)

        def evac_at(stage):
            return NC * EVAC_ROUNDS.index(stage)

        def buffer_free(eng, c):
            if c >= 2:
                eng.wait_ge(s_h, c - 1)
                turned = sum(x in TURNED for x in SPREADS[:(c - 2) // NC])
                if SPREADS[(c - 2) // NC] in TURNED:
                    eng.wait_ge(s_trans, NC * turned + (c - 2) % NC + 1)
                split = sum(x in SPLIT for x in SPREADS[:(c - 2) // NC])
                if SPREADS[(c - 2) // NC] in SPLIT:
                    eng.wait_ge(s_r1, NC * split + (c - 2) % NC + 1)
                stored = sum(x % 2 == c % 2 and SPREADS[x // NC] in STORED for x in range(c - 1))
                eng.wait_ge(s_stored[c % 2], 16 * stored)

        def chunk_rows(dram_rows, j):
            b, n = CHUNKS[j]
            return dram_rows[b * PT:(b + n) * PT, :].rearrange("(t p) f -> p t f", p=PT)

        def span_registers(eng, name, ranges):
            return ([eng.alloc_register(f"{name}_packed{e}") for e in range(ranges)],
                    [eng.alloc_register(f"{name}_end{e}") for e in range(2)])

        def load_ranges(eng, regs, bounds, at):
            eng.reg_load(regs[0], bounds[0:1, bass.ds(at, len(regs[0]))])

        def unpack_range(eng, regs, n, most):
            low, high = regs[1]
            eng.reg_alu(low, regs[0][n], PACK_BITS, ALU.logical_shift_right)
            eng.reg_alu(high, regs[0][n], PACK - 1, ALU.bitwise_and)
            return eng.snap(low, min_val=0, max_val=most - 1), eng.snap(high, min_val=1, max_val=most)

        def all_windows(eng, regs, body):
            with eng.Fori(0, NW // WL) as i:
                load_ranges(eng, regs, window_bounds, i * WL)
                for q in range(WL):
                    body(i * WL + q, q, i * (WL // 2) + q // 2 + 1)
            load_ranges(eng, regs, window_bounds, TAIL)
            for w in range(TAIL, NW):
                body(w, w - TAIL, w // 2 + 1)

        @block.sync
        def _(sp):
            sp.dma_start(dst_nat, a["dst_rows"].rearrange("g (u e) -> g u e", e=U * PT)).then_inc(s_dst, 16)
            sp.dma_start(src_i, a["src_t"]).then_inc(s_edges, 16)
            sp.dma_start(dst_i, a["dst_t"]).then_inc(s_edges, 16)
            sp.dma_start(typ_i, a["typ_t"]).then_inc(s_edges, 16)
            sp.wait_ge(s_unit_f, 1)
            for c in range(2):
                sp.dma_start(unit_scratch[c].rearrange("(g u) -> g u", g=NG), unit_f[:, c, :]).then_inc(s_scratch_out[0], 16)
            sp.wait_ge(s_scratch_out[0], 32)
            sp.dma_start(unit_lo, unit_scratch[0:1, :].to_broadcast([H, NU])).then_inc(s_scratch_in[0], 16)
            sp.dma_start(unit_hi, unit_scratch[1:2, :].to_broadcast([H, NU])).then_inc(s_scratch_in[0], 16)
            sp.wait_ge(s_group_i, 1)
            sp.dma_start(group_scratch, group_i).then_inc(s_scratch_out[1], 16)
            sp.wait_ge(s_window_i, 1)
            for h in range(2):
                sp.dma_start(window_scratch[h * H:(h + 1) * H, :], window_i[:, h:h + 1]).then_inc(s_scratch_out[2], 16)
            sp.wait_ge(s_scratch_out[2], 32)
            sp.dma_start(window_bounds, window_scratch.rearrange("(a w) c -> a (w c)", a=1)).then_inc(s_scratch_in[2], 16)
            sp.wait_ge(s_scratch_out[1], 16)
            sp.dma_start(group_bounds[:], group_scratch.rearrange("(a g) c -> a (g c)", a=1)).then_inc(s_scratch_in[1], 16)
            sp.wait_ge(s_typed, 1)
            sp.dma_start(typed_index, typed_i).then_inc(s_typed_out, 16)
            sp.wait_ge(s_typed_out, 16)

            def load_index(r, src):
                sp.dma_start(index, src).then_inc(s_index[r], 16)

            def store_spread(stage):
                for i, j in enumerate(ORDER):
                    c = spread_at(stage) + i
                    sp.wait_ge(s_h, c + 1)
                    n = CHUNKS[j][1]
                    sp.dma_start(chunk_rows(node_table, j),
                                 rows[0:PT, c % 2, 0:n * H].rearrange("p (t f) -> p t f", f=H)).then_inc(s_stored[c % 2], 16)

            def sage_index(r, stage):
                over = sp.value_load(over_flag[0:1, 0:1], min_val=0, max_val=1)
                with sp.If(over > 0):
                    sp.wait_ge(s_p3, before(stage, SPLIT) + NC)
                    load_index(r, a["src_t"])
                with sp.Else():
                    sp.nop()

            def final(n, r):
                for i in range(NC + 2):
                    if i < NC:
                        j, c = ORDER[i], NC * n + i
                        if i >= 2:
                            sp.wait_ge(s_resid, c - 1)
                        m = CHUNKS[j][1]
                        x_from = a["x"] if n == 0 else x_dram
                        if i == 0 and ROUNDS[r] == SAGE:
                            sp.wait_ge(s_summed, r + 1)
                        sp.dma_start(tmp[0:PT, c % 2, 0:m * H].rearrange("p (t f) -> p t f", f=H),
                                     chunk_rows(x_from, j)).then_inc(s_x_old[c % 2], 16)
                    if i >= 2:
                        j, c = ORDER[i - 2], NC * n + i - 2
                        b, m = CHUNKS[j]
                        sp.wait_ge(s_resid, c + 1)
                        sp.dma_start(chunk_rows(out if n == 3 else x_dram, j), x_rows[:, b:b + m, :]).then_inc(s_x_out[n], 16)

            def store_typed(layer):
                view = typed_table.rearrange("(b p t) f -> b p (t f)", p=PT, t=T)
                for b in range(NB):
                    c = NB * layer + b
                    sp.wait_ge(s_tab_a, c + 1)
                    sp.wait_ge(s_tab_v, c + 1)
                    sp.dma_start(view[b], table_stage[:, c % 2, :]).then_inc(s_staged[c % 2], 16)

            sp.wait_ge(s_over, 1)
            sp.dma_start(x_rows, a["x"].rearrange("(t p) f -> p t f", p=PT)).then_inc(s_x, 16)
            store_spread("N0")
            sage_index(0, "N0")
            store_spread("M0")
            sage_index(1, "M0")
            store_spread("M1")
            sage_index(2, "M1")
            final(0, 2)
            sp.wait_ge(s_lin, lin_at("F0") + NC)
            sp.dma_start(w_layer[:], a["w_gru0"]).then_inc(s_layer_w[1], 16)
            sp.dma_start(b_rows[0:1, :], a["b_out"]).then_inc(s_layer_w[1], 16)
            sp.dma_start(w_types, a["w_types0"]).then_inc(s_types_w[0], 16)
            sp.wait_ge(s_proj, NC)
            sp.dma_start(w_single[:], a["w_out"]).then_inc(s_single_w[1], 16)
            sp.wait_ge(s_over, 1)
            load_index(3, typed_index)
            store_typed(0)
            sp.wait_ge(s_tab, NB)
            sp.dma_start(w_types, a["w_types1"]).then_inc(s_types_w[1], 16)
            sp.wait_ge(s_gates, len(HALVES))
            sp.dma_start(w_layer[:], a["w_gru1"]).then_inc(s_layer_w[2], 16)
            sp.wait_ge(s_gru, len(HALVES))
            load_index(4, typed_index)
            store_typed(1)
            sp.wait_ge(s_gates, 2 * len(HALVES))
            sp.dma_start(w_layer[:], a["w_sage2"]).then_inc(s_layer_w[3], 16)
            final(1, 4)
            sp.wait_ge(s_lin, lin_at("F1") + NC)
            for n in range(3):
                sp.dma_start(b_rows[32 * n:32 * n + 1, :], a["b_sage2"][n:n + 1, :]).then_inc(s_layer_w[3], 16)
            sp.dma_start(w_single[:], a["w_last"]).then_inc(s_single_w[2], 16)
            store_spread("N2")
            sage_index(5, "N2")
            store_spread("M5")
            sage_index(6, "M5")
            store_spread("M6")
            sage_index(7, "M6")
            final(2, 7)
            load_index(8, a["src_t"])
            store_spread("N3")
            sp.wait_ge(s_pre, spread_at("N3") + NC)
            sp.wait_ge(s_x_out[2], 16 * NC)
            sp.dma_start(weight, a["weight_t"]).then_inc(s_index[8], 16)
            sp.wait_ge(s_summed, 9)
            final(3, 8)
            sp.wait_ge(s_x_out[3], 16 * NC)

        @block.gpsimd
        def _(pool):
            pool.iota(key_ids, pattern=[[1, KEYS]], base=0, channel_multiplier=0,
                      allow_small_or_imprecise_dtypes=True).then_inc(s_ids, 1)
            pool.iota(block_ids[:], pattern=[[1, PT]], base=0, channel_multiplier=0,
                      allow_small_or_imprecise_dtypes=True).then_inc(s_ids, 1)
            pool.iota(block_base[:], pattern=[[PT, NB]], base=0, channel_multiplier=0,
                      allow_small_or_imprecise_dtypes=True).then_inc(s_ids, 1)
            pool.iota(window_base, pattern=[[KEYS, NW]], base=0, channel_multiplier=0,
                      allow_small_or_imprecise_dtypes=True).then_inc(s_ids, 1)
            pool.iota(window_id, pattern=[[H, 2]], base=0, channel_multiplier=1,
                      allow_small_or_imprecise_dtypes=True).then_inc(s_ids, 1)
            pool.iota(unit_up, pattern=[[1, NU]], base=1, channel_multiplier=0,
                      allow_small_or_imprecise_dtypes=True).then_inc(s_ids, 1)
            pool.iota(unit_down, pattern=[[-1, NU]], base=NU, channel_multiplier=0,
                      allow_small_or_imprecise_dtypes=True).then_inc(s_ids, 1)
            pool.iota(lo_ids, pattern=[[1, PT]], base=0, channel_multiplier=0,
                      allow_small_or_imprecise_dtypes=True).then_inc(s_ids, 1)
            pool.memset(ident[:], 0.0).then_inc(s_pool, 1)
            pool.wait_ge(s_pool, 1)
            pool.affine_select(out=ident[:], in_=ident[:], compare_op=ALU.not_equal, fill=1.0, base=0,
                               pattern=[[-1, H]], channel_multiplier=1).then_inc(s_ident, 1)
            copies = pool.alloc_register("ring_copies")
            pool.reg_mov(copies, 1)
            free = [pool.alloc_register(f"slot_freed{g}") for g in range(SLOTS)]
            for g in range(SLOTS):
                pool.reg_mov(free[g], 1)
            landed = [pool.alloc_register(f"slot_landed{g}") for g in range(SLOTS)]
            for g in range(SLOTS):
                pool.reg_mov(landed[g], 0)

            def gather(r, table):
                pool.wait_ge(s_index[r], 32 if ROUNDS[r] == WEIGHTED else 16)
                with pool.Fori(0, NG // SLOTS) as i:
                    for g in range(SLOTS):
                        if g < 2:
                            for slot in (2 * g, 2 * g + 1):
                                pool.wait_ge(s_gathered[slot], pool.snap(landed[slot], min_val=0))
                                pool.reg_add(landed[slot], landed[slot], 16 * G)
                            lo = 2 * g * G
                            pool.tensor_copy(ring[:, lo:lo + 2 * G],
                                             index[:, bass.ds(i * (SLOTS * G) + lo, 2 * G)]).then_inc(s_ring, 1)
                        if g % 2 == 0:
                            pool.wait_ge(s_ring, pool.snap(copies, min_val=1))
                            pool.reg_add(copies, copies, 1)
                        pool.wait_ge(s_free[g], pool.snap(free[g], min_val=1))
                        pool.reg_add(free[g], free[g], 1)
                        for u in range(G):
                            pool.indirect_dma_start(
                                msg[g][:, u, :], None, table,
                                bass.IndirectOffsetOnAxis(ap=ring[:, g * G + u:g * G + u + 1], axis=0),
                            ).then_inc(s_gathered[g], 16)

            def rows_in_table(stage):
                for q in range(2):
                    mine = sum((spread_at(stage) + i) % 2 == q for i in range(NC))
                    pool.wait_ge(s_stored[q], 16 * (stores_before(stage, q) + mine))

            def sage(r, stage):
                over = pool.value_load(over_flag[0:1, 0:1], min_val=0, max_val=1)
                with pool.If(over > 0):
                    rows_in_table(stage)
                    pool.wait_ge(s_p3, before(stage, SPLIT) + NC)
                    pool.wait_ge(s_turned, before(stage, TURNED) + NC)
                    gather(r, node_table)
                with pool.Else():
                    pool.nop()

            pool.wait_ge(s_over, 1)
            sage(0, "N0")
            sage(1, "M0")
            sage(2, "M1")
            for layer in range(2):
                for q in range(2):
                    done = sum(c % 2 == q for c in range(NB * (layer + 1)))
                    pool.wait_ge(s_staged[q], 16 * done)
                gather(3 + layer, typed_table)
            sage(5, "N2")
            sage(6, "M5")
            sage(7, "M6")
            rows_in_table("N3")
            gather(8, node_table)

        @block.vector
        def _(dve):
            chain = [0]

            def link(ins):
                chain[0] += 1
                ins.then_inc(s_dve, 1)
                dve.wait_ge(s_dve, chain[0])

            v = nc.vector

            def layer_norm_stats(blocks):
                for t in blocks:
                    last = v.bn_stats(stats[:, t, :], x_rows[:, t, :])
                return last

            def layer_norm_moments():
                for t in range(NB):
                    last = v.bn_aggr(moments[:, t, :], stats[:, t, :])
                last.then_inc(s_std_in, 1)

            v.memset(zeros[:], 0.0)
            v.memset(zero_keys, 0.0)
            v.memset(eps_col[:], EPS)
            v.memset(over_col[:], -255.0)
            v.memset(ones_bf, 1.0)
            v.memset(ones[:], 1.0).then_inc(s_const, 1)

            dve.wait_ge(s_dst, 16)
            v.tensor_reduce(unit_f[:, 0, :], dst_nat, AX.X, ALU.min)
            link(v.tensor_reduce(unit_f[:, 1, :], dst_nat, AX.X, ALU.max))
            v.tensor_reduce(group_f[:, 0:1], unit_f[:, 0, :], AX.X, ALU.min)
            link(v.tensor_reduce(group_f[:, 1:2], unit_f[:, 1, :], AX.X, ALU.max))
            link(v.tensor_scalar(unit_f, unit_f, -(WN - 1) / 2.0, 1.0 / WN, ALU.add, ALU.mult))
            link(v.tensor_copy(unit_i, unit_f))
            v.tensor_copy(unit_f, unit_i).then_inc(s_unit_f, 1)
            half = (PT - 1) / 2.0
            link(v.tensor_scalar(group_f[:, 0:1], group_f[:, 0:1], -half, 1.0 / PT, ALU.add, ALU.mult))
            link(v.tensor_scalar(group_f[:, 1:2], group_f[:, 1:2], PT - half, 1.0 / PT, ALU.add, ALU.mult))
            v.tensor_scalar(group_b[:, 0:1], group_f[:, 0:1], 0.0, NB - 1.0, ALU.max, ALU.min)
            link(v.tensor_scalar(group_b[:, 1:2], group_f[:, 1:2], 1.0, float(NB), ALU.max, ALU.min))
            link(v.tensor_copy(group_f, group_b))
            v.scalar_tensor_tensor(group_i, group_f[:, 0:1], float(PACK), group_f[:, 1:2], ALU.mult, ALU.add).then_inc(s_group_i, 1)

            dve.wait_ge(s_edges, 48)
            link(v.tensor_scalar(hi_f, src_i, -half, 1.0 / PT, ALU.add, ALU.mult))
            link(v.tensor_copy(hi_i, hi_f))
            v.tensor_copy(dst_f[:], dst_i)
            link(v.tensor_copy(hi_f, hi_i))
            v.scalar_tensor_tensor(lo_f, hi_f, -float(PT), src_i, ALU.mult, ALU.add)
            v.scalar_tensor_tensor(key_f, dst_f[:], float(NB), hi_f, ALU.mult, ALU.add)
            v.scalar_tensor_tensor(typed_i, src_i, float(T), typ_i, ALU.mult, ALU.add).then_inc(s_typed, 1)

            dve.wait_ge(s_ids, 8)
            dve.wait_ge(s_scratch_in[0], 32)
            for h in range(2):
                w = window_id[:, h:h + 1]
                link(v.tensor_scalar(lies[h], unit_lo, w, None, ALU.is_le))
                link(v.scalar_tensor_tensor(met[h], unit_hi, w, lies[h], ALU.is_ge, ALU.mult))
                link(v.tensor_tensor(lies[h], met[h], unit_up, ALU.mult))
                v.tensor_reduce(window_f[:, h, 1:2], lies[h], AX.X, ALU.max)
                link(v.tensor_tensor(met[h], met[h], unit_down, ALU.mult))
                link(v.tensor_reduce(window_f[:, h, 0:1], met[h], AX.X, ALU.max))
            link(v.tensor_scalar(window_f[:, :, 0], window_f[:, :, 0], -1.0, float(NU), ALU.mult, ALU.add))
            link(v.tensor_scalar(window_f[:, :, 0], window_f[:, :, 0], float(NU - 1), None, ALU.min))
            link(v.scalar_tensor_tensor(window_f[:, :, 1], window_f[:, :, 0], 1.0, window_f[:, :, 1], ALU.add, ALU.max))
            link(v.tensor_scalar(window_f, window_f, float(U), None, ALU.mult))
            v.scalar_tensor_tensor(window_i, window_f[:, :, 0], float(PACK), window_f[:, :, 1], ALU.mult, ALU.add).then_inc(s_window_i, 1)

            units = dve.alloc_register("dve_units")
            place = dve.alloc_register("dve_place")
            spans = span_registers(dve, "dve_window", WL)
            group_spans = span_registers(dve, "dve_group", SLOTS)
            dve.reg_mov(units, 0)
            dve.wait_ge(s_typed, 1)
            dve.wait_ge(s_scratch_in[2], 16)

            def key_onehots(w, q, pair):
                low, high = unpack_range(dve, spans, q, NTILE)
                with dve.Fori(low, high, U) as k:
                    dve.reg_add(units, units, 1)
                    dve.wait_ge(s_unit_used, dve.snap(units, min_val=1))
                    dve.reg_alu(place, units, RING - 1, ALU.bitwise_and)
                    at_ring = dve.snap(place, min_val=0, max_val=RING - 1)
                    v.tensor_tensor(
                        lo_hot[:, bass.ds(at_ring * (U * H), U * H)].rearrange("p (u c) -> p u c", u=U)[:, :, 0:PT],
                        lo_ids[:, None, :].to_broadcast([PT, U, PT]),
                        lo_wide[:, bass.ds(k, U), None].to_broadcast([PT, U, PT]), ALU.is_equal)
                    v.scalar_tensor_tensor(
                        key_hot[:, bass.ds(at_ring * (U * KEYS), U * KEYS)].rearrange("p (u c) -> p u c", u=U),
                        key_ids[:, None, :].to_broadcast([PT, U, KEYS]), window_base[:, bass.ds(w, 1)],
                        key_wide[:, bass.ds(k, U), None].to_broadcast([PT, U, KEYS]),
                        ALU.add, ALU.is_equal).then_inc(s_unit, 1)

            all_windows(dve, spans, key_onehots)

            for q in range(2):
                dve.wait_ge(s_bank_free[q], (NW + 1 - q) // 2 + 1)
            v.tensor_reduce(over_col[:], over_parts, AX.X, ALU.add).then_inc(s_over_sum, 1)
            dve.wait_ge(s_over_sum, 2)
            v.tensor_scalar(over_flag[:], bank(7)[0:1, 0:1], 0.5, None, ALU.is_gt).then_inc(s_over, 1)
            dve.wait_ge(s_x, 16)
            link(layer_norm_stats(range(NB)))
            layer_norm_moments()
            dve.wait_ge(s_deg_turned, NC)
            link(v.tensor_scalar(rdeg[:], bank(0)[0:PT, 0:NB], 1.0, None, ALU.max))
            v.reciprocal(rdeg[:], rdeg[:]).then_inc(s_rdeg, 1)

            pairs = [dve.alloc_register(f"dve_pairs{h}") for h in range(2)]
            for h in range(2):
                dve.reg_mov(pairs[h], 0)
            dve.wait_ge(s_scratch_in[1], 16)

            def onehots(r):
                with dve.Fori(0, NG // SLOTS) as i:
                    load_ranges(dve, group_spans, group_bounds, i * SLOTS)
                    for g in range(SLOTS):
                        h = g % 2
                        lo, edges = h * G, bass.ds(i * (SLOTS * G) + g * G, G)
                        low, high = unpack_range(dve, group_spans, g, NB)
                        with dve.Fori(low, high) as b:
                            dve.reg_add(pairs[h], pairs[h], 1)
                            dve.wait_ge(s_onehot_used[h], dve.snap(pairs[h], min_val=1))
                            base = block_base[:, bass.ds(b, 1)]
                            mine = dst_f[:, edges, None].to_broadcast([PT, G, PT])
                            ids = block_ids[:, None, :].to_broadcast([PT, G, PT])
                            last = v.scalar_tensor_tensor(onehot[:, lo:lo + G, :], ids, base, mine, ALU.add, ALU.is_equal)
                            if ROUNDS[r] == WEIGHTED:
                                link_dynamic(last, h)
                                scale = weight[:, edges, None].to_broadcast([PT, G, PT])
                                last = v.tensor_tensor(onehot[:, lo:lo + G, :], onehot[:, lo:lo + G, :], scale, ALU.mult)
                            last.then_inc(s_onehot[h], 1)

            raw = dve.alloc_register("dve_raw_onehots")
            dve.reg_mov(raw, 0)

            def link_dynamic(ins, h):
                ins.then_inc(s_raw, 1)
                dve.reg_add(raw, raw, 1)
                dve.wait_ge(s_raw, dve.snap(raw, min_val=1))

            def sage_onehots(r, stage):
                over = dve.value_load(over_flag[0:1, 0:1], min_val=0, max_val=1)
                with dve.If(over > 0):
                    dve.wait_ge(s_p3, before(stage, SPLIT) + NC)
                    onehots(r)
                with dve.Else():
                    dve.nop()

            def evac(stage, r, i):
                j = ORDER[i]
                n, c = CHUNKS[j][1], evac_at(stage) + i
                dve.wait_ge(s_summed, r + 1)
                if i >= 2:
                    dve.wait_ge(s_lin, lin_at(stage) + i - 1)
                v.tensor_copy(agg[:, i % 2, 0:n * PT].rearrange("p (b c) -> p b c", c=PT), acc(j)).then_inc(s_evac, 1)

            def residue1(stage, i):
                c, n = spread_at(stage) + i, CHUNKS[ORDER[i]][1]
                b = CHUNKS[ORDER[i]][0]
                dve.wait_ge(s_h, c + 1)
                if before(stage, SPLIT) + i >= 2:
                    dve.wait_ge(s_p3, before(stage, SPLIT) + (i - 1 if i >= 2 else 0))
                v.tensor_tensor(tmp[0:PT, i % 2, 0:n * H], rows[0:PT, c % 2, 0:n * H],
                                parts[:, 0, b:b + n, :].rearrange("p b f -> p (b f)"), ALU.subtract).then_inc(s_r1, 1)

            def residue2(stage, i):
                b, n = CHUNKS[ORDER[i]]
                dve.wait_ge(s_p2, before(stage, SPLIT) + i + 1)
                v.tensor_tensor(parts[:, 2, b:b + n, :].rearrange("p b f -> p (b f)"), tmp[0:PT, i % 2, 0:n * H],
                                parts[:, 1, b:b + n, :].rearrange("p b f -> p (b f)"), ALU.subtract).then_inc(s_p3, 1)

            def combine(i, c, into):
                b, n = CHUNKS[ORDER[i]]
                for t in range(n):
                    o = slice(t * H, (t + 1) * H)
                    last = v.scalar_tensor_tensor(into[:, o], bank(ORDER[i])[0:PT, o], rdeg[:, b + t:b + t + 1],
                                                  into[:, o], ALU.mult, ALU.add)
                return last

            def sage_mid(r, stage):
                sage_onehots(r, SPREADS[SPREADS.index(stage) - 1])
                evac(stage, r, 0)
                for i in range(NC + 2):
                    if i + 1 < NC:
                        evac(stage, r, i + 1)
                    if i < NC:
                        c = spread_at(stage) + i
                        dve.wait_ge(s_root, ROOTS.index(stage) * NC + i + 1)
                        combine(i, c, rows[0:PT, c % 2]).then_inc(s_pre, 1)
                    if 1 <= i <= NC:
                        residue1(stage, i - 1)
                    if i >= 2:
                        residue2(stage, i - 2)

            def layer_norm(n):
                stage = f"N{n}"
                dve.wait_ge(s_std, n + 1)
                link(v.reciprocal(rstd[:], std[:]))
                split = stage in SPLIT
                for i in range(NC + 2 * split):
                    if i < NC:
                        b, m = CHUNKS[ORDER[i]]
                        c = spread_at(stage) + i
                        buffer_free(dve, c)
                        for t in range(m):
                            last = v.tensor_scalar(rows[0:PT, c % 2, t * H:(t + 1) * H], x_rows[:, b + t, :],
                                                   moments[:, b + t, 0:1], rstd[:, b + t:b + t + 1],
                                                   ALU.subtract, ALU.mult)
                        last.then_inc(s_pre, 1)
                    if split and 1 <= i <= NC:
                        residue1(stage, i - 1)
                    if split and i >= 2:
                        residue2(stage, i - 2)

            def final(n, r, stage):
                kind = ROUNDS[r]
                if kind != TYPED:
                    evac(stage, r, 0)
                for i in range(NC):
                    if kind != TYPED and i + 1 < NC:
                        evac(stage, r, i + 1)
                    b, m = CHUNKS[ORDER[i]]
                    c = NC * n + i
                    x_new = x_rows[:, b:b + m, :].rearrange("p b f -> p (b f)")
                    if n < 3 and i:
                        dve.wait_ge(s_resid, c)
                        bb, mm = CHUNKS[ORDER[i - 1]]
                        layer_norm_stats(range(bb, bb + mm))
                    dve.wait_ge(s_lin, lin_at(stage) + i + 1)
                    x_wait = sum(x % 2 == c % 2 for x in range(c + 1))
                    dve.wait_ge(s_x_old[c % 2], 16 * x_wait)
                    if kind == SAGE:
                        dve.wait_ge(s_root, ROOTS.index(stage) * NC + i + 1)
                        link(combine(i, c, rows[0:PT, c % 2]))
                        v.tensor_tensor(x_new, rows[0:PT, c % 2, 0:m * H], tmp[0:PT, c % 2, 0:m * H], ALU.add).then_inc(s_resid, 1)
                    else:
                        src = root_bank(i) if kind == TYPED else bank(ORDER[i])
                        v.tensor_tensor(x_new, src[0:PT, 0:m * H], tmp[0:PT, c % 2, 0:m * H], ALU.add).then_inc(s_resid, 1)
                if n < 3:
                    dve.wait_ge(s_resid, NC * (n + 1))
                    link(layer_norm_stats(range(b, b + m)))
                    layer_norm_moments()

            def typed_half(layer):
                for b in range(NB):
                    c = NB * layer + b
                    dve.wait_ge(s_tab, c + 1)
                    if c >= 2:
                        dve.wait_ge(s_staged[c % 2], 16 * (c // 2))
                    v.tensor_copy(table_stage[:, c % 2, BANK:2 * BANK], table_bank(b, 1)[0:PT, :]).then_inc(s_tab_v, 1)

            def gru(layer, r):
                dve.wait_ge(s_summed, r + 1)
                for j in range(0, NC, 2):
                    b, n = CHUNKS[j]
                    v.tensor_copy(aggT[:, b:b + n, :], acc(j)).then_inc(s_agg_v, 1)
                c0 = len(HALVES) * layer

                def first_part(c):
                    b, m = HALVES[c]
                    q, n = c % GRU_STEPS, m * PT
                    dve.wait_ge(s_act1, c0 + c + 1)
                    link(v.tensor_tensor(gate_r[q][:, 0:n], gate_r[q][:, 0:n], gate_n[q][:, 0:n], ALU.mult))
                    v.tensor_tensor(gate_r[q][:, 0:n], gate_r[q][:, 0:n], bank(2 * (c % GRU_PAIRS) + 1)[:, 0:n],
                                    ALU.add).then_inc(s_dve1, 1)

                def second_part(c):
                    b, m = HALVES[c]
                    q, n = c % GRU_STEPS, m * PT
                    h = hT[:, b:b + m, 0:PT]
                    gz, gn = (g[q][:, 0:n].rearrange("p (b c) -> p b c", c=PT) for g in (gate_z, gate_n))
                    dve.wait_ge(s_act2, c0 + c + 1)
                    link(v.tensor_tensor(h, h, gn, ALU.subtract))
                    link(v.tensor_tensor(h, h, gz, ALU.mult))
                    link(v.tensor_tensor(h, h, gn, ALU.add))
                    v.tensor_scalar(h, h, 0.0, None, ALU.max).then_inc(s_gru, 1)

                for c in range(len(HALVES) + 1):
                    if c < len(HALVES):
                        first_part(c)
                    if c:
                        second_part(c - 1)

            dve.wait_ge(s_small, 16 * 2)
            v.tensor_tensor(b_rz[:], b_gru[:, :, 0, 0:2], b_gru[:, :, 1, 0:2], ALU.add).then_inc(s_const, 1)
            layer_norm(0)
            sage_mid(0, "M0")
            sage_mid(1, "M1")
            sage_onehots(2, "M1")
            final(0, 2, "F0")
            layer_norm(1)
            for layer in range(2):
                typed_half(layer)
                onehots(3 + layer)
                gru(layer, 3 + layer)
            final(1, 4, "F1")
            layer_norm(2)
            sage_mid(5, "M5")
            sage_mid(6, "M6")
            sage_onehots(7, "M6")
            final(2, 7, "F2")
            layer_norm(3)
            dve.wait_ge(s_index[8], 32)
            onehots(8)
            final(3, 8, "F3")

        @block.tensor
        def _(pe):
            mm = nc.tensor.matmul
            pe.wait_ge(s_const, 1)
            pe.sem_inc(s_unit_used, RING)
            for h in range(2):
                pe.sem_inc(s_onehot_used[h], 1)
            for slot in range(SLOTS):
                pe.sem_inc(s_free[slot], 1)

            units = pe.alloc_register("pe_units")
            spans = span_registers(pe, "pe_window", WL)
            group_spans = span_registers(pe, "pe_group", SLOTS)
            place = pe.alloc_register("pe_place")
            taken = pe.alloc_register("pe_windows")
            pe.reg_mov(units, 0)
            pe.wait_ge(s_scratch_in[2], 16)

            def window(w, n, wait):
                low, high = unpack_range(pe, spans, n, NTILE)
                q = n % 2
                o = bank(q)[0:PT, 0:KEYS]
                pe.wait_ge(s_bank_free[q], wait)
                mm(o, zeros[:, 0:PT], zero_keys, start=True, stop=False)
                with pe.Fori(low, high, U) as k:
                    pe.reg_add(units, units, 1)
                    pe.wait_ge(s_unit, pe.snap(units, min_val=1))
                    pe.reg_alu(place, units, RING - 1, ALU.bitwise_and)
                    at_ring = pe.snap(place, min_val=0, max_val=RING - 1)
                    for u in range(U):
                        last = mm(o, lo_hot[:, bass.ds(at_ring * (U * H) + u * H, PT)],
                                  key_hot[:, bass.ds(at_ring * (U * KEYS) + u * KEYS, KEYS)], start=False, stop=False)
                    last.then_inc(s_unit_used, 1)
                mm(o, zeros[:, 0:PT], zero_keys, start=False, stop=True).then_inc(s_window, 1)

            pe.sem_inc(s_bank_free[0], 1)
            pe.sem_inc(s_bank_free[1], 1)
            all_windows(pe, spans, window)

            def turn_degrees(j):
                b, n = CHUNKS[j]
                pe.wait_ge(s_deg_row, j + 1)
                for t in range(n):
                    last = mm(bank(0)[0:PT, b + t:b + t + 1], deg_row[:, j % 2, t * PT:(t + 1) * PT], ones[0:1, 0:1],
                              start=True, stop=True)
                last.then_inc(s_deg_turned, 1)

            pe.wait_ge(s_over_sum, 1)
            mm(bank(7)[0:1, 0:1], over_col[:], ones[:, 0:1], start=True, stop=True).then_inc(s_over_sum, 1)
            pe.wait_ge(s_counted, NW)
            for j, (b, n) in enumerate(CHUNKS):
                o = bank(1 + j % 2)[0:1, 0:n * PT]
                if j >= 2:
                    pe.wait_ge(s_deg_row, j - 1)
                for t in range(NB):
                    last = mm(o, ones_bf[:, 0:1], counts[:, t, b * PT:(b + n) * PT], start=t == 0, stop=t == NB - 1)
                last.then_inc(s_deg, 1)
                if j:
                    turn_degrees(j - 1)
            turn_degrees(NC - 1)

            pairs = [pe.alloc_register(f"pe_pairs{h}") for h in range(2)]
            landed = [pe.alloc_register(f"pe_landed{g}") for g in range(SLOTS)]
            for g in range(SLOTS):
                pe.reg_mov(landed[g], 16 * G)
            for h in range(2):
                pe.reg_mov(pairs[h], 0)
            pe.wait_ge(s_scratch_in[1], 16)

            def open_sums():
                for j in range(NC):
                    mm(bank(j).rearrange("p (b c) -> p b c", c=H), zeros[:], zeros[:, None, :].to_broadcast([1, 4, H]),
                       start=True, stop=False)

            def close_sums():
                for j in range(NC):
                    last = mm(bank(j).rearrange("p (b c) -> p b c", c=H), zeros[:], zeros[:, None, :].to_broadcast([1, 4, H]),
                              start=False, stop=True)
                last.then_inc(s_summed, 1)

            def sum_gathered():
                with pe.Fori(0, NG // SLOTS) as i:
                    load_ranges(pe, group_spans, group_bounds, i * SLOTS)
                    for g in range(SLOTS):
                        h = g % 2
                        low, high = unpack_range(pe, group_spans, g, NB)
                        pe.wait_ge(s_gathered[g], pe.snap(landed[g], min_val=1))
                        pe.reg_add(landed[g], landed[g], 16 * G)
                        with pe.Fori(low, high) as b:
                            pe.reg_add(pairs[h], pairs[h], 1)
                            pe.wait_ge(s_onehot[h], pe.snap(pairs[h], min_val=1))
                            for u in range(G):
                                last = mm(psum[:, bass.ds(b * H, PT)], msg[g][:, u, :], onehot[:, h * G + u, :],
                                          start=False, stop=False)
                            last.then_inc(s_onehot_used[h], 1)
                        mm(spare, zeros[:, 0:1], zeros[:, 0:1], start=True, stop=True).then_inc(s_free[g], 1)

            def sum_dense(stage):
                for i, j in enumerate(ORDER):
                    b, n = CHUNKS[j]
                    pe.wait_ge(s_p3, before(stage, SPLIT) + i + 1)
                    with pe.Fori(b, b + n) as t:
                        for k in range(3):
                            part = parts[:, k, bass.ds(t, 1), :].rearrange("p b f -> p (b f)")
                            for jj, (bb, m) in enumerate(CHUNKS):
                                mm(acc(jj), part,
                                   counts[:, bass.ds(t, 1), bb * PT:(bb + m) * PT].rearrange("p a (b c) -> p (a b) c", c=PT),
                                   start=False, stop=False)

            def sage(r, stage):
                over = pe.value_load(over_flag[0:1, 0:1], min_val=0, max_val=1)
                pe.wait_ge(s_turned, before(stage, TURNED) + NC)
                open_sums()
                with pe.If(over > 0):
                    sum_gathered()
                with pe.Else():
                    sum_dense(stage)
                close_sums()

            def transpose_rows(stage, i):
                c, n = spread_at(stage) + i, CHUNKS[ORDER[i]][1]
                pe.wait_ge(s_h, c + 1)
                for t in range(n):
                    last = nc.tensor.transpose(turned_bank(i)[:, t * PT:(t + 1) * PT], rows[0:PT, c % 2, t * H:(t + 1) * H],
                                               ident[0:PT, 0:PT])
                last.then_inc(s_trans, 1)

            def linear(stage, i, w, bias, banks_free):
                j = ORDER[i]
                b, n = CHUNKS[j]
                if w[1] is not None:
                    banks_free(i)
                    for t in range(n):
                        o = root_bank(i)[0:PT, t * H:(t + 1) * H]
                        mm(o, hT[:, b + t, 0:PT], w[1], start=True, stop=False)
                        last = mm(o, ones[32 * bias:32 * bias + 1, 0:PT], b_rows[32 * bias:32 * bias + 1, :], start=False, stop=True)
                if w[0] is not None:
                    pe.wait_ge(s_evac, evac_at(stage) + i + 1)
                    for t in range(n):
                        last = mm(bank(j)[0:PT, t * H:(t + 1) * H], agg[:, i % 2, t * PT:(t + 1) * PT], w[0],
                                  start=True, stop=True)
                last.then_inc(s_lin, 1)

            def w_of(n):
                return w_layer[:, n * H:(n + 1) * H]

            def sage_mid(r, stage, n):
                def banks_free(i):
                    if i >= 2:
                        pe.wait_ge(s_root, ROOTS.index(stage) * NC + i - 1)
                    if i == 2:
                        pe.wait_ge(s_turned, before(stage, TURNED) + 1)
                    if i == 1:
                        pe.wait_ge(s_pre, spread_at(stage) + 1)

                for i in range(NC + 1):
                    if i < NC:
                        linear(stage, i, (w_of(2 * n), w_of(2 * n + 1)), n, banks_free)
                    if i:
                        transpose_rows(stage, i - 1)

            def final(n, stage, w, bias):
                def banks_free(i):
                    if stage == "F1":
                        pe.wait_ge(s_gru, len(HALVES) + 2 * i + 1)
                    if i >= 2 or i == 1 and stage != "F1":
                        pe.wait_ge(s_resid, NC * n + (i - 1 if i >= 2 else 1))

                for i in range(NC):
                    linear(stage, i, w, bias, banks_free)

            def turn_norm(stage):
                for i in range(NC):
                    transpose_rows(stage, i)

            def typed_products(layer):
                pe.wait_ge(s_types_w[layer], 16)
                for b in range(NB):
                    c = NB * layer + b
                    if layer:
                        pe.wait_ge(s_gru, min(b // 2 + 2, len(HALVES)))
                        if b == 1:
                            pe.wait_ge(s_dve1, len(HALVES))
                    if b >= 4:
                        pe.wait_ge(s_tab_a, c - 3)
                        pe.wait_ge(s_tab_v, c - 3)
                    for q in range(2):
                        last = mm(table_bank(b, q)[0:PT, :], hT[:, b, 0:PT], w_types[:, q * BANK:(q + 1) * BANK],
                                  start=True, stop=True)
                    last.then_inc(s_tab, 1)

            def gru(layer):
                pe.wait_ge(s_agg_v, (NC + 1) // 2 * (layer + 1))
                pe.wait_ge(s_agg_a, NC // 2 * (layer + 1))
                pe.wait_ge(s_layer_w[1 + layer], 32 if layer == 0 else 16)
                c0 = len(HALVES) * layer
                for c, (b, m) in enumerate(HALVES):
                    n = m * PT
                    if c >= GRU_PAIRS:
                        pe.wait_ge(s_dve1, c0 + c - GRU_PAIRS + 1)
                    x, h = aggT[:, b:b + m, :], hT[:, b:b + m, 0:PT]
                    rz, nn = bank(2 * (c % GRU_PAIRS)), bank(2 * (c % GRU_PAIRS) + 1)
                    for g in range(2):
                        o = rz[:, g * 2 * PT:g * 2 * PT + n]
                        mm(o, w_layer[:, g * H:(g + 1) * H], x, start=True, stop=False)
                        mm(o, w_layer[:, (3 + g) * H:(4 + g) * H], h, start=False, stop=True)
                    mm(nn[:, 0:n], w_of(2), x, start=True, stop=True)
                    mm(nn[:, 2 * PT:2 * PT + n], w_of(5), h, start=True, stop=True).then_inc(s_gates, 1)

            pe.wait_ge(s_ident, 1)
            pe.wait_ge(s_layer_w[0], 64)
            pe.wait_ge(s_rdeg, 1)
            turn_norm("N0")
            sage(0, "N0")
            sage_mid(0, "M0", 0)
            sage(1, "M0")
            sage_mid(1, "M1", 1)
            sage(2, "M1")
            final(0, "F0", (w_of(4), w_of(5)), 2)
            turn_norm("N1")
            pe.wait_ge(s_turned, before("N1", TURNED) + NC)
            pe.wait_ge(s_single_w[0], 16)
            for i, (b, m) in enumerate(CHUNKS):
                mm(bank(i)[:, 0:m * PT], w_single[:], hT[:, b:b + m, 0:PT], start=True, stop=True).then_inc(s_proj, 1)
            pe.wait_ge(s_projed, NC)
            for layer in range(2):
                typed_products(layer)
                pe.wait_ge(s_tab_a, NB * (layer + 1))
                pe.wait_ge(s_tab_v, NB * (layer + 1))
                open_sums()
                sum_gathered()
                close_sums()
                gru(layer)
            pe.wait_ge(s_single_w[1], 16)
            final(1, "F1", (None, w_single[:]), 0)
            turn_norm("N2")
            pe.wait_ge(s_layer_w[3], 64)
            sage(5, "N2")
            sage_mid(5, "M5", 0)
            sage(6, "M5")
            sage_mid(6, "M6", 1)
            sage(7, "M6")
            final(2, "F2", (w_of(4), w_of(5)), 2)
            pe.wait_ge(s_resid, NC * 3)
            pe.wait_ge(s_single_w[2], 16)
            open_sums()
            sum_gathered()
            close_sums()
            final(3, "F3", (w_single[:], None), None)

        @block.scalar
        def _(act):
            act.dma_start(w_layer[:], a["w_sage0"]).then_inc(s_layer_w[0], 16)
            for n in range(3):
                act.dma_start(b_rows[32 * n:32 * n + 1, :], a["b_sage0"][n:n + 1, :]).then_inc(s_layer_w[0], 16)
            act.dma_start(b_proj[:], a["b_proj"]).then_inc(s_small, 16)
            act.dma_start(b_gru[:], a["b_gru"]).then_inc(s_small, 16)
            act.dma_start(w_single[:], a["w_proj"]).then_inc(s_single_w[0], 16)
            fn = nc.scalar.activation

            act.wait_ge(s_const, 1)

            def take_window(w, q, n):
                o = bank(q)[0:PT, 0:n * NB]
                fn(counts[:, :, bass.ds(w * WN, n)].rearrange("p h d -> p d h"),
                   o.rearrange("p (d h) -> p d h", h=NB), ACT.Copy).then_inc(s_counted, 1)
                fn(o, o, ACT.Relu, bias=over_col[:], accum_out=over_parts[:, bass.ds(w, 1)]).then_inc(s_bank_free[q], 1)

            with act.Fori(0, (NW - 1) // 2) as i:
                for q in range(2):
                    act.wait_ge(s_window, i * 2 + q + 1)
                    take_window(i * 2 + q, q, WN)
            for w in range((NW - 1) // 2 * 2, NW):
                act.wait_ge(s_window, w + 1)
                take_window(w, w % 2, min(WN, N - w * WN))

            for j, (b, n) in enumerate(CHUNKS):
                act.wait_ge(s_deg, j + 1)
                if j >= 2:
                    act.wait_ge(s_deg_turned, j - 1)
                fn(deg_row[:, j % 2, 0:n * PT], bank(1 + j % 2)[0:1, 0:n * PT], ACT.Copy).then_inc(s_deg_row, 1)

            def root(n):
                act.wait_ge(s_std_in, n + 1)
                fn(std[:], moments[:, :, 1], ACT.Sqrt, bias=eps_col[:]).then_inc(s_std, 1)

            def take_root(stage, i, c):
                act.wait_ge(s_lin, lin_at(stage) + i + 1)
                n = CHUNKS[ORDER[i]][1] * H
                fn(rows[0:PT, c % 2, 0:n], root_bank(i)[0:PT, 0:n], ACT.Copy).then_inc(s_root, 1)

            def final_roots(n, stage):
                free_at = spread_at(f"N{n + 1}")
                buffer_free(act, free_at)
                buffer_free(act, free_at + 1)
                for i in range(NC):
                    c = NC * n + i
                    if i >= 2:
                        act.wait_ge(s_resid, c - 1)
                    take_root(stage, i, c)

            def spread(stage):
                split, turned = stage in SPLIT, stage in TURNED
                inner = stage[0] == "M"
                if inner:
                    buffer_free(act, spread_at(stage))
                    take_root(stage, 0, spread_at(stage))
                    buffer_free(act, spread_at(stage) + 1)
                    take_root(stage, 1, spread_at(stage) + 1)
                for i in range(NC + 1):
                    if i < NC:
                        b, n = CHUNKS[ORDER[i]]
                        c = spread_at(stage) + i
                        act.wait_ge(s_pre, c + 1)
                        mine = rows[0:PT, c % 2, 0:n * H]
                        if split:
                            fn(parts[:, 0, b:b + n, :].rearrange("p b f -> p (b f)"), mine, ACT.Relu)
                        fn(mine, mine, ACT.Relu).then_inc(s_h, 1)
                    if i:
                        b, n = CHUNKS[ORDER[i - 1]]
                        if turned:
                            if i == 1 and stage[0] == "N" and stage != "N0":
                                act.wait_ge(s_x_out[int(stage[1]) - 1], 16 * NC)
                            if i == 1 and stage[0] == "N":
                                act.wait_ge(s_pre, spread_at(stage) + 1)
                            act.wait_ge(s_trans, before(stage, TURNED) + i)
                            fn(hT[:, b:b + n, 0:PT], turned_bank(i - 1)[:, 0:n * PT].rearrange("p (b c) -> p b c", c=PT),
                               ACT.Copy).then_inc(s_turned, 1)
                        if split:
                            act.wait_ge(s_r1, before(stage, SPLIT) + i)
                            fn(parts[:, 1, b:b + n, :].rearrange("p b f -> p (b f)"), tmp[0:PT, (i - 1) % 2, 0:n * H],
                               ACT.Copy).then_inc(s_p2, 1)
                        if inner and i + 1 < NC:
                            buffer_free(act, spread_at(stage) + i + 1)
                            take_root(stage, i + 1, spread_at(stage) + i + 1)

            def typed_half(layer):
                for b in range(NB):
                    c = NB * layer + b
                    act.wait_ge(s_tab, c + 1)
                    if c >= 2:
                        act.wait_ge(s_staged[c % 2], 16 * (c // 2))
                    fn(table_stage[:, c % 2, 0:BANK], table_bank(b, 0)[0:PT, :], ACT.Copy).then_inc(s_tab_a, 1)

            def gru(layer, r):
                act.wait_ge(s_summed, r + 1)
                for j in range(1, NC, 2):
                    b, n = CHUNKS[j]
                    fn(aggT[:, b:b + n, :], acc(j), ACT.Copy).then_inc(s_agg_a, 1)
                c0 = len(HALVES) * layer

                def gate(c):
                    n = HALVES[c][1] * PT
                    q = c % GRU_STEPS
                    rz, nn = bank(2 * (c % GRU_PAIRS)), bank(2 * (c % GRU_PAIRS) + 1)
                    act.wait_ge(s_gates, c0 + c + 1)
                    if c >= GRU_STEPS:
                        act.wait_ge(s_gru, c0 + c - GRU_STEPS + 1)
                    fn(gate_r[q][:, 0:n], rz[:, 0:n], ACT.Sigmoid, bias=b_rz[:, layer, 0:1])
                    fn(gate_z[q][:, 0:n], rz[:, 2 * PT:2 * PT + n], ACT.Sigmoid, bias=b_rz[:, layer, 1:2])
                    fn(gate_n[q][:, 0:n], nn[:, 2 * PT:2 * PT + n], ACT.Identity,
                       bias=b_gru[:, layer, 1, 2:3]).then_inc(s_act1, 1)

                def candidate(c):
                    n = HALVES[c][1] * PT
                    act.wait_ge(s_dve1, c0 + c + 1)
                    fn(gate_n[c % GRU_STEPS][:, 0:n], gate_r[c % GRU_STEPS][:, 0:n], ACT.Tanh,
                       bias=b_gru[:, layer, 0, 2:3]).then_inc(s_act2, 1)

                for c in range(len(HALVES) + 1):
                    if c < len(HALVES):
                        gate(c)
                    if c:
                        candidate(c - 1)

            root(0)
            spread("N0")
            spread("M0")
            spread("M1")
            final_roots(0, "F0")
            root(1)
            spread("N1")
            for j, (b, m) in enumerate(CHUNKS):
                act.wait_ge(s_proj, j + 1)
                fn(hT[:, b:b + m, 0:PT], bank(j)[:, 0:m * PT].rearrange("p (b c) -> p b c", c=PT), ACT.Relu,
                   bias=b_proj[:]).then_inc(s_projed, 1)
            act.wait_ge(s_const, 2)
            for layer in range(2):
                typed_half(layer)
                gru(layer, 3 + layer)
            root(2)
            spread("N2")
            spread("M5")
            spread("M6")
            final_roots(2, "F2")
            root(3)
            spread("N3")


def laid_out(i):
    import numpy as np

    def tiles(v):
        return v.reshape(NTILE, PT).T

    i = {k: np.asarray(v) for k, v in i.items()}
    sage0 = [i[f"L0_gnn_W{k}{n}"].T for n in range(3) for k in "lr"]
    sage2 = [i[f"L2_gnn_W{k}"][n] for n in range(3) for k in "lr"]
    put = {
        "dst_rows": i["dst"].reshape(NG, G * PT), "dst_t": tiles(i["dst"]), "src_t": tiles(i["src"]),
        "typ_t": tiles(i["edge_type_8"]), "weight_t": tiles(i["edge_weight"]), "x": i["x"],
        "w_sage0": np.concatenate(sage0, 1), "w_sage2": np.concatenate(sage2, 1),
        "b_sage0": np.stack([i[f"L0_gnn_bl{n}"] for n in range(3)]), "b_sage2": i["L2_gnn_b"],
        "b_out": i["L1_gnn_out_b"][None], "b_proj": i["L1_gnn_node_proj_b"][:, None],
        "b_gru": np.stack([i["L1_gnn_gru_bih"], i["L1_gnn_gru_bhh"]]).reshape(2, 2, 3, H).transpose(3, 1, 0, 2),
        "w_proj": i["L1_gnn_node_proj_w"].T, "w_out": i["L1_gnn_out_w"].T, "w_last": i["L3_gnn_W"].T,
    }
    for n in range(2):
        put[f"w_gru{n}"] = np.concatenate([i["L1_gnn_gru_wih"][n].T, i["L1_gnn_gru_whh"][n].T], 1)
        put[f"w_types{n}"] = i["L1_gnn_edge_W"][n].transpose(2, 0, 1).reshape(H, T * H)
    return {k: np.ascontiguousarray(v) for k, v in put.items()}


def kernel(**inputs):
    import concourse.bacc as bacc
    from concourse.bass_utils import run_bass_kernel_spmd

    arrays = laid_out(inputs)
    nc = bacc.Bacc("TRN2", target_bir_lowering=False, num_devices=1)
    aps = {k: nc.dram_tensor(f"in_{k}", v.shape, mybir.dt.from_np(v.dtype), kind="ExternalInput").ap()
           for k, v in arrays.items()}
    out = nc.dram_tensor("out_x", (N, H), F32, kind="ExternalOutput").ap()
    gnn_program(nc, aps, out)
    got = run_bass_kernel_spmd(nc, [{f"in_{k}": v for k, v in arrays.items()}], core_ids=[0])
    return got.results[0]["out_x"]
```
